# Optimizing a Trainium2 kernel written in Bass

```python
import numpy as np
import jax
import jax.numpy as jnp

def _softmax(x, axis=-1):
    return jax.nn.softmax(x, axis=axis)
def _gelu(x):
    return jax.nn.gelu(x, approximate=True)
def _silu(x):
    return jax.nn.silu(x)
def _sigmoid(x):
    return jax.nn.sigmoid(x)
def _layernorm(x, axis=-1, eps=1e-5):
    m = jnp.mean(x, axis=axis, keepdims=True)
    v = jnp.var(x, axis=axis, keepdims=True)
    return (x - m) / jnp.sqrt(v + eps)
def _scatter_add(tgt, idx, src, axis=0):
    return tgt.at[idx].add(src)
def _segment_sum(src, seg, n):
    return jax.ops.segment_sum(src, seg, n)

kernel_name = 'mk_conv_seq_d2_conv_nchw64_9b43a4'

def setup_inputs(seed: int = 0):
    np.random.seed(seed)
    _w = jnp.asarray
    def _rec_inputs():
        import jax
        import jax.numpy as jnp
        _gk = jax.random.key(seed)
        x = -0.0005207 + 1.001 * jax.random.normal(jax.random.fold_in(_gk, 1), (8, 64, 64, 64), jnp.float32)
        return x
    x = _rec_inputs()
    def _L0_conv_setup():
        import jax, jax.numpy as jnp
        import numpy as np
        INTER = 32

        def conv1x1(x, w, b):
            return jnp.einsum('bchw,oc->bohw', x, w) + b[None, :, None, None]
        key = jax.random.key(seed)
        ks = jax.random.split(key, 12)
        B, C, H, W = (8, 64, 64, 64)
        inter = INTER
        s_in = 1.0 / np.sqrt(C)
        s_int = 1.0 / np.sqrt(inter)
        return {'x': jax.random.normal(ks[0], (B, C, H, W), jnp.float32), 'g_w': jax.random.normal(ks[1], (inter, C), jnp.float32) * s_in, 'g_b': jax.random.normal(ks[2], (inter,), jnp.float32) * s_in, 'theta_w': jax.random.normal(ks[3], (inter, C), jnp.float32) * s_in, 'theta_b': jax.random.normal(ks[4], (inter,), jnp.float32) * s_in, 'phi_w': jax.random.normal(ks[5], (inter, C), jnp.float32) * s_in, 'phi_b': jax.random.normal(ks[6], (inter,), jnp.float32) * s_in, 'W_w': jax.random.normal(ks[7], (C, inter), jnp.float32) * s_int, 'W_b': jax.random.normal(ks[8], (C,), jnp.float32) * s_int, 'Wz1_w': jax.random.normal(ks[9], (C, inter), jnp.float32) * s_int, 'Wz1_b': jax.random.normal(ks[10], (C,), jnp.float32) * s_int, 'mb': jax.random.normal(ks[11], (inter, 256), jnp.float32)}
    _L0_conv_all = _L0_conv_setup()
    _L0_conv_in = {k: v for k, v in _L0_conv_all.items() if k in ('g_w', 'g_b', 'theta_w', 'theta_b', 'phi_w', 'phi_b', 'W_w', 'W_b', 'Wz1_w', 'Wz1_b', 'mb', )}
    del _L0_conv_all

    def _L1_conv_setup():
        import jax, jax.numpy as jnp
        import numpy as np
        key = jax.random.key(seed)
        k1, k2 = jax.random.split(key)
        B, C, H, W = (8, 64, 64, 64)
        x = jax.random.normal(k1, (B, C, H, W), dtype=jnp.float32)
        stdv = 1.0 / np.sqrt(C)
        weight = jax.random.uniform(k2, (C, C), dtype=jnp.float32, minval=-stdv, maxval=stdv)
        return {'x': x, 'weight': weight}
    _L1_conv_all = _L1_conv_setup()
    _L1_conv_in = {k: v for k, v in _L1_conv_all.items() if k in ('weight', )}
    del _L1_conv_all

    return {
        "x": x,
        "L0_conv_g_w": _L0_conv_in["g_w"],
        "L0_conv_g_b": _L0_conv_in["g_b"],
        "L0_conv_theta_w": _L0_conv_in["theta_w"],
        "L0_conv_theta_b": _L0_conv_in["theta_b"],
        "L0_conv_phi_w": _L0_conv_in["phi_w"],
        "L0_conv_phi_b": _L0_conv_in["phi_b"],
        "L0_conv_W_w": _L0_conv_in["W_w"],
        "L0_conv_W_b": _L0_conv_in["W_b"],
        "L0_conv_Wz1_w": _L0_conv_in["Wz1_w"],
        "L0_conv_Wz1_b": _L0_conv_in["Wz1_b"],
        "L0_conv_mb": _L0_conv_in["mb"],
        "L1_conv_weight": _L1_conv_in["weight"],
    }

def reference(x, L0_conv_g_w, L0_conv_g_b, L0_conv_theta_w, L0_conv_theta_b, L0_conv_phi_w, L0_conv_phi_b, L0_conv_W_w, L0_conv_W_b, L0_conv_Wz1_w, L0_conv_Wz1_b, L0_conv_mb, L1_conv_weight):
    import jax
    import jax.numpy as jnp
    def _L0_conv_ref(x, g_w, g_b, theta_w, theta_b, phi_w, phi_b, W_w, W_b, Wz1_w, Wz1_b, mb):
        import jax, jax.numpy as jnp
        import numpy as np
        INTER = 32

        def conv1x1(x, w, b):
            return jnp.einsum('bchw,oc->bohw', x, w) + b[None, :, None, None]
        b, c, h, w = x.shape
        inter = g_w.shape[0]
        g_x = conv1x1(x, g_w, g_b).reshape(b, inter, -1)
        theta_x = conv1x1(x, theta_w, theta_b).reshape(b, inter, -1)
        phi_x = conv1x1(x, phi_w, phi_b).reshape(b, inter, -1)
        f = jnp.einsum('bcn,bcm->bnm', theta_x, phi_x)
        f_div_C = jax.nn.softmax(f, axis=-1)
        y = jnp.einsum('bnm,bcm->bcn', f_div_C, g_x)
        y = y.reshape(b, inter, h, w)
        W_y = conv1x1(y, W_w, W_b)
        f1 = jnp.einsum('bcn,ck->bnk', phi_x, mb)
        scale = jnp.float32(int(inter) ** (-0.5))
        f_div_C1 = jax.nn.softmax(f1 * scale, axis=-1)
        y1 = jnp.einsum('bnk,ck->bcn', f_div_C1, mb)
        y1 = y1.reshape(b, inter, h, w)
        W_y1 = conv1x1(y1, Wz1_w, Wz1_b)
        return W_y + x + W_y1

    def _L1_conv_ref(x, weight):
        import jax, jax.numpy as jnp
        import numpy as np
        B, C, H, W = x.shape
        N = H * W
        xf = x.reshape(B, C, N)
        g_x = jnp.transpose(xf, (0, 2, 1))
        f = jnp.einsum('bic,bcj->bij', g_x, xf)
        adj = jax.nn.softmax(f, axis=-1)
        support = jnp.einsum('bnc,cd->bnd', g_x, weight)
        y = jnp.einsum('bij,bjc->bic', adj, support)
        y = jnp.transpose(y, (0, 2, 1)).reshape(B, C, H, W)
        return y + x

    def _gn(v, G=32, eps=1e-5):
        B_, C_, H_, W_ = v.shape
        g = v.reshape(B_, G, C_ // G, H_, W_)
        m = jnp.mean(g, axis=(2, 3, 4), keepdims=True)
        s = jnp.var(g, axis=(2, 3, 4), keepdims=True)
        return ((g - m) / jnp.sqrt(s + eps)).reshape(v.shape)

    def _ln_c(v, eps=1e-6):
        m = jnp.mean(v, axis=1, keepdims=True)
        s = jnp.var(v, axis=1, keepdims=True)
        return (v - m) / jnp.sqrt(s + eps)

    def _ln_t(v, eps=1e-5):
        m = jnp.mean(v, axis=-1, keepdims=True)
        s = jnp.var(v, axis=-1, keepdims=True)
        return (v - m) / jnp.sqrt(s + eps)

    def _to_tokens(v):
        B_, C_, H_, W_ = v.shape
        return v.reshape(B_, C_, H_ * W_).transpose(0, 2, 1)
    def _from_tokens(t, like):
        B_, C_, H_, W_ = like.shape
        return t.transpose(0, 2, 1).reshape(B_, C_, H_, W_)

    x = _L0_conv_ref(x, L0_conv_g_w, L0_conv_g_b, L0_conv_theta_w, L0_conv_theta_b, L0_conv_phi_w, L0_conv_phi_b, L0_conv_W_w, L0_conv_W_b, L0_conv_Wz1_w, L0_conv_Wz1_b, L0_conv_mb)
    x = _L1_conv_ref(x, L1_conv_weight)
    return x


_drawn_inputs = setup_inputs


def setup_inputs(seed=0):
    import zlib

    import numpy as np

    out = dict(_drawn_inputs(seed))
    spreads = {}
    factors = {'L0_conv_phi_b': 2.844}
    for name, (base, spread) in spreads.items():
        noise = np.random.default_rng([zlib.crc32(name.encode()), seed]).standard_normal(out[name].shape)
        drawn = base * np.exp(spread * noise) if base else spread * noise
        out[name] = jnp.asarray(drawn.astype(out[name].dtype))
    for name, factor in factors.items():
        out[name] = (out[name] * factor).astype(out[name].dtype)
    return out
```

```python
from contextlib import ExitStack

import concourse.bass as bass
from concourse import mybir

ALU = mybir.AluOpType
ACT = mybir.ActivationFunctionType
AX_X = mybir.AxisListType.X
F32 = mybir.dt.float32
F16 = mybir.dt.float16
U32 = mybir.dt.uint32
RMAX = bass.bass_isa.ReduceOp.max

P = 128
GROUP = 512
EXPONENT = 0x7F800000
TINY = 1e-30


def non_local_then_graph(nc, x, weights_in, wstat_in, bcol_in, out_w_in, out_b_in, g_bias_in,
                         bank_in, bank_t_in, ident_in, out):
    B, C, N = x.shape
    I = C // 2
    NG = N // GROUP
    NK = N // GROUP
    NC = N // P
    PER = GROUP // P
    BANK = bank_in.shape[1]
    BC = BANK // P
    S0 = 3 * I
    R0 = S0 + 2
    R1 = C + 2
    LANES = [PER * BC, PER]
    WIDE = [I + 1, C + 1]
    T = [NC + BC, NC]
    PER_IMAGE = NG * (T[0] + T[1])
    BANK_SCALE = float(I) ** -0.5
    assert S0 <= 96 and NC == 32 and BC == 2 and PER == 4

    def tile0(b, layer, g):
        return b * PER_IMAGE + (NG * T[0] if layer else 0) + g * T[layer]

    def group_no(b, layer, g):
        return b * (2 * NG) + layer * NG + g

    with ExitStack() as ctx:
        def sb(name, shape, dt):
            return ctx.enter_context(nc.sbuf_tensor(name, shape, dt))

        def psum(name, shape, dt):
            return ctx.enter_context(nc.psum_tensor(name, shape, dt))

        def sem(name):
            return ctx.enter_context(nc.semaphore(name))

        w_proj = sb("w_proj", [C, 2 * S0 + I + C], F32)
        w_stat = sb("w_stat", [P, 2, C], F32)
        b_col = sb("b_col", [P, 2], F32)
        w_out = sb("w_out", [C, 2 * C], F32)
        b_out2 = sb("b_out2", [P, 2], F32)
        b_out = sb("b_out", [P, 1], F32)
        g_bias = sb("g_bias", [P, PER, I], F32)
        bank = sb("bank", [P, BANK], F32)
        bank_val = sb("bank_val", [P, BC, I + 1], F32)
        ident = sb("ident", [P, P], F32)
        ident16 = sb("ident16", [P, P], F16)
        ones2 = sb("ones2", [2, P], F16)
        zero16 = sb("zero16", [32, GROUP], F16)
        x_sb = sb("x_sb", [P, N], F32)
        full32 = sb("full32", [S0, 2, 2, GROUP], F32)
        q0 = sb("q0", [P, N], F16)
        k0 = sb("k0", [P, N], F16)
        bank_stack = sb("bank_stack", [P, BANK], F16)
        bank32 = sb("bank32", [P, BANK], F32)
        v0 = sb("v0", [P, NC, I + 1], F32)
        x1 = sb("x1", [P, N], F32)
        q1a = sb("q1a", [P, N], F16)
        k1a = sb("k1a", [P, N], F16)
        q1b = sb("q1b", [P, N], F16)
        k1b = sb("k1b", [P, N], F16)
        v1 = sb("v1", [P, NC, C + 1], F32)
        out_sb = sb("out_sb", [C, N], F32)
        w_exp = sb("w_exp", [P, PER, GROUP], F32)
        w_bank = sb("w_bank", [P, BC, GROUP], F32)
        bank_max = sb("bank_max", [2, GROUP], F16)
        max_part = sb("max_part", [P, PER, NK], F32)
        neg_max = sb("neg_max", [P, 2 * PER], F32)
        max_cols = sb("max_cols", [P, 2 * PER, 2], F16)
        recip = sb("recip", [P, 2 * PER], F32)
        y_norm = sb("y_norm", [P, PER, C], F32)
        y_t = sb("y_t", [C, GROUP], F32)
        x1_max = sb("x1_max", [P, NG], F32)
        stat = sb("stat", [P, 5], F32)
        stat_all = sb("stat_all", [P, 5], F32)
        peak = sb("peak", [P, 1], F32)
        peak_all = sb("peak_all", [P, 1], F32)
        bound = sb("bound", [P, 2], F32)
        pow_up = sb("pow_up", [P, 2], F32)
        pow_dn = sb("pow_dn", [P, 2], F32)
        scale = sb("scale", [P, 2], F32)
        inv = sb("inv", [P, 2], F32)
        bank_s = sb("bank_s", [P, 2], F32)
        b_scaled = sb("b_scaled", [P, 2], F32)
        logit = sb("logit", [P, 3], F32)
        scale1 = sb("scale1", [P, 1], F32)

        row_ps = psum("row_ps", [P, 2, GROUP], F32)
        col_ps = psum("col_ps", [P, 2, GROUP], F32)
        acc_ps = psum("acc_ps", [P, GROUP], F32)
        max_ps = psum("max_ps", [P, GROUP], F32)
        yt_ps = psum("yt_ps", [P, GROUP], F32)
        proj_ps = psum("proj_ps", [P, GROUP], F32)

        weights_loaded = sem("weights_loaded")
        x_loaded = sem("x_loaded")
        out_stored = sem("out_stored")
        consts_set = sem("consts_set")
        stats_ready = sem("stats_ready")
        stats_all_ready = sem("stats_all_ready")
        bank_step = sem("bank_step")
        peak_ready = sem("peak_ready")
        peak_seen = sem("peak_seen")
        peak_all_ready = sem("peak_all_ready")
        scale_step = sem("scale_step")
        scale0_ready = sem("scale0_ready")
        scale1_ready = sem("scale1_ready")
        theta_psum_ready = sem("theta_psum_ready")
        phi_psum_ready = sem("phi_psum_ready")
        v_psum_ready = sem("v_psum_ready")
        theta_ready = sem("theta_ready")
        phi_ready = sem("phi_ready")
        v0_ready = sem("v0_ready")
        v1_ready = sem("v1_ready")
        hi_ready = sem("hi_ready")
        stack0_ready = sem("stack0_ready")
        k1a_ready = sem("k1a_ready")
        hi1_ready = sem("hi1_ready")
        lo1_ready = sem("lo1_ready")
        row_ready = sem("row_ready")
        row_free = sem("row_free")
        col_ready = sem("col_ready")
        exp_ready = sem("exp_ready")
        exp_free = sem("exp_free")
        neg_max_ready = sem("neg_max_ready")
        max_hi_ready = sem("max_hi_ready")
        max_cols_ready = sem("max_cols_ready")
        max_psum_ready = sem("max_psum_ready")
        max_rows_ready = sem("max_rows_ready")
        recip_ready = sem("recip_ready")
        y_ready = sem("y_ready")
        yt_psum_ready = sem("yt_psum_ready")
        yt_done = sem("yt_done")
        proj_psum_ready = sem("proj_psum_ready")
        x1_ready = sem("x1_ready")
        x1_max_ready = sem("x1_max_ready")

        WEIGHT_LOADS = [
            (w_proj[:, :], weights_in[:, :]), (w_stat[:, :, :], wstat_in[:, :, :]),
            (b_col[:, :], bcol_in[:, :]), (w_out[:, :], out_w_in[:, :]),
            (b_out2[:, :], out_b_in[:, :]), (g_bias[:, :, :], g_bias_in[:, :, :]),
            (bank[:, :], bank_in[:, :]), (bank_val[:, :, 0:I], bank_t_in[:, :, :]),
            (ident[:, :], ident_in[:, :]),
        ]
        ROWS = [R0, P]
        q_stack, k_stack = [q0, q1a], [k0, k1a]

        block = ctx.enter_context(nc.Block())

        @block.sync
        def _(sp):
            def load_image(b):
                for half in range(2):
                    sp.dma_start(x_sb[half * C:(half + 1) * C, :],
                                 x[bass.ds(b, 1)].rearrange("a c n -> (a c) n")).then_inc(x_loaded, 16)

            def store_group(b, g):
                sp.wait_ge(yt_done, group_no(b, 1, g) + 1)
                sp.dma_start(out[bass.ds(b, 1), :, bass.ds(g * GROUP, GROUP)].rearrange("a c n -> (a c) n"),
                             out_sb[:, bass.ds(g * GROUP, GROUP)]).then_inc(out_stored, 16)

            load_image(0)
            for dst, src in WEIGHT_LOADS:
                sp.dma_start(dst, src).then_inc(weights_loaded, 16)
            with sp.Fori(0, B - 1) as b:
                sp.wait_ge(x1_ready, (b + 1) * NG)
                load_image(b + 1)
                with sp.Fori(0, NG) as g:
                    store_group(b, g)
            with sp.Fori(0, NG) as g:
                store_group(B - 1, g)
            sp.wait_ge(out_stored, B * NG * 16)

        @block.tensor
        def _(pe):
            def project_layer0(b):
                pe.wait_ge(x_loaded, (b + 1) * 32)
                pe.wait_ge(yt_done, group_no(b, 0, 0))
                pe.wait_ge(v1_ready, b * NG)
                for j in range(NK):
                    cols = slice(j * GROUP, (j + 1) * GROUP)
                    pe.wait_ge(theta_ready, b * NK + j)
                    pe.matmul(max_ps[0:S0, :], w_proj[:, 0:S0], x_sb[0:C, cols],
                              start=True, stop=True).then_inc(theta_psum_ready, 1)
                    pe.wait_ge(phi_ready, b * NK + j)
                    pe.matmul(yt_ps[0:S0, :], w_proj[:, S0:2 * S0], x_sb[0:C, cols],
                              start=True, stop=True).then_inc(phi_psum_ready, 1)
                    pe.wait_ge(v0_ready, b * NK + j)
                    for i in range(PER):
                        tok = slice((j * PER + i) * P, (j * PER + i + 1) * P)
                        mm = pe.matmul(proj_ps[:, i * I:(i + 1) * I], x_sb[0:C, tok],
                                       w_proj[:, 2 * S0:2 * S0 + I], start=True, stop=True)
                    mm.then_inc(v_psum_ready, 1)

            def project_layer1(b):
                pe.wait_ge(x1_ready, (b + 1) * NG)
                for j in range(NK):
                    pe.wait_ge(v1_ready, b * NK + j)
                    for i in range(PER):
                        tok = slice((j * PER + i) * P, (j * PER + i + 1) * P)
                        mm = pe.matmul(proj_ps[:, i * C:(i + 1) * C], x1[0:C, tok],
                                       w_proj[:, 2 * S0 + I:], start=True, stop=True)
                    mm.then_inc(v_psum_ready, 1)

            def row_tile(b, layer, g, kt, i):
                pe.wait_ge(row_free, tile0(b, layer, g) + kt * PER + i + 1)
                queries = bass.ds(g * GROUP + i * P, P)
                keys = bass.ds(kt * GROUP, GROUP)
                if layer == 0:
                    mm = pe.matmul(row_ps[:, i % 2, :], q0[0:S0, queries], k0[0:S0, keys],
                                   start=True, stop=True)
                else:
                    pe.matmul(row_ps[:, i % 2, :], q1a[:, queries], k1a[:, keys], start=True, stop=False)
                    mm = pe.matmul(row_ps[:, i % 2, :], q1b[0:R1, queries], k1b[0:R1, keys],
                                   start=False, stop=True)
                mm.then_inc(row_ready, 1)

            def row_bank(b, g):
                for t in range(BC):
                    pe.wait_ge(row_free, tile0(b, 0, g) + NC + t + 1)
                    for i in range(2):
                        mm = pe.matmul(row_ps[:, t, i * BANK:(i + 1) * BANK],
                                       k0[0:S0, bass.ds(g * GROUP + (2 * t + i) * P, P)],
                                       bank_stack[0:S0, :], start=True, stop=True)
                    mm.then_inc(row_ready, 1)

            def col_tile(layer, g, kt, c):
                keys = bass.ds(kt * GROUP + c * P, P)
                queries = bass.ds(g * GROUP, GROUP)
                if layer == 0:
                    mm = pe.matmul(col_ps[:, c % 2, :], k0[0:R0, keys], q0[0:R0, queries],
                                   start=True, stop=True)
                else:
                    pe.matmul(col_ps[:, c % 2, :], k1a[:, keys], q1a[:, queries], start=True, stop=False)
                    mm = pe.matmul(col_ps[:, c % 2, :], k1b[0:R1, keys], q1b[0:R1, queries],
                                   start=False, stop=True)
                mm.then_inc(col_ready, 1)

            def col_bank(g, c):
                pe.matmul(col_ps[:, c % 2, :], bank_stack[0:S0, c * P:(c + 1) * P],
                          k0[0:S0, bass.ds(g * GROUP, GROUP)], start=True, stop=False)
                pe.matmul(col_ps[:, c % 2, :], ones2[:, :], bank_max[:, :],
                          start=False, stop=True).then_inc(col_ready, 1)

            def weigh(layer, kt, c, last):
                w, v = WIDE[layer], (v0, v1)[layer]
                for i in range(PER):
                    mm = pe.matmul(acc_ps[:, i * w:(i + 1) * w], w_exp[:, c, i * P:(i + 1) * P],
                                   v[:, bass.ds(kt * PER + c, 1), :].rearrange("p a w -> p (a w)"),
                                   start=False, stop=last and c == PER - 1, skip_group_check=True)
                mm.then_inc(exp_free, 1)

            def weigh_bank(c):
                w = WIDE[0]
                for i in range(PER):
                    s = PER + i
                    mm = pe.matmul(acc_ps[:, s * w:(s + 1) * w], w_bank[:, c, i * P:(i + 1) * P],
                                   bank_val[:, c, :], start=False, stop=c == BC - 1, skip_group_check=True)
                mm.then_inc(exp_free, 1)

            def start_group(b, layer, g):
                n = group_no(b, layer, g)
                pe.wait_ge(max_cols_ready, n + 1)
                row = (S0, C)[layer]
                for i in range(PER):
                    mm = pe.matmul(max_ps[row:row + 2, i * P:(i + 1) * P], max_cols[:, i, :], ident16[:, :],
                                   start=True, stop=True, skip_group_check=True)
                if layer == 0:
                    for i in range(PER):
                        mm = pe.matmul(max_ps[0:2, i * P:(i + 1) * P], max_cols[:, PER + i, :], ident16[:, :],
                                       start=True, stop=True, skip_group_check=True)
                mm.then_inc(max_psum_ready, 1)
                pe.wait_ge(y_ready, n)
                pe.matmul(acc_ps[:, 0:LANES[layer] * WIDE[layer]], zero16[:, 0:P],
                          zero16[:, 0:LANES[layer] * WIDE[layer]], start=True, stop=False,
                          skip_group_check=True)
                pe.wait_ge(max_rows_ready, n + 1)
                col_tile(layer, g, 0, 0)
                col_tile(layer, g, 0, 1)

            def key_tile(b, layer, g, kt, rows_of, last):
                for c in range(PER):
                    if rows_of is not None:
                        row_tile(b, layer, rows_of, kt, c)
                    pe.wait_ge(exp_ready, tile0(b, layer, g) + kt * PER + c + 1)
                    if not last or c < PER - 2:
                        col_tile(layer, g, kt, c + 2)
                    elif layer == 0:
                        col_bank(g, c - (PER - 2))
                    weigh(layer, kt, c, last)

            def group(b, layer, g, rows_of):
                with pe.Fori(0, NK - 1) as kt:
                    key_tile(b, layer, g, kt, rows_of, False)
                key_tile(b, layer, g, NK - 1, rows_of, True)
                if layer == 0:
                    if rows_of is not None:
                        row_bank(b, rows_of)
                    for c in range(BC):
                        pe.wait_ge(exp_ready, tile0(b, 0, g) + NC + c + 1)
                        weigh_bank(c)

            def finish_group(b, layer, g):
                n = group_no(b, layer, g)
                pe.wait_ge(y_ready, n + 1)
                pe.wait_ge(yt_done, n)
                for i in range(PER):
                    mm = pe.matmul(yt_ps[0:C, i * P:(i + 1) * P], y_norm[:, i, :], ident[:, :],
                                   start=True, stop=True)
                mm.then_inc(yt_psum_ready, 1)
                if layer == 0:
                    pe.wait_ge(yt_done, n + 1)
                    pe.matmul(proj_ps[:, :], w_out[:, :], y_t[:, :], start=True, stop=True)\
                        .then_inc(proj_psum_ready, 1)

            def layer_passes(b, layer):
                with pe.Fori(0, NK) as kt:
                    if layer == 0:
                        pe.wait_ge(stack0_ready, b * NK + kt + 1)
                    else:
                        pe.wait_ge(lo1_ready, b * NK + kt + 1)
                        pe.wait_ge(hi1_ready, b * NK + kt + 1)
                    for i in range(PER):
                        row_tile(b, layer, 0, kt, i)
                if layer == 0:
                    row_bank(b, 0)
                    pe.wait_ge(v0_ready, (b + 1) * NK)
                else:
                    pe.wait_ge(v1_ready, (b + 1) * NK)
                start_group(b, layer, 0)
                with pe.Fori(0, NG - 1) as g:
                    group(b, layer, g, g + 1)
                    start_group(b, layer, g + 1)
                    finish_group(b, layer, g)
                group(b, layer, NG - 1, None)
                finish_group(b, layer, NG - 1)

            pe.wait_ge(weights_loaded, len(WEIGHT_LOADS) * 16)
            pe.wait_ge(consts_set, 11)
            pe.wait_ge(bank_step, 4)
            with pe.Fori(0, B) as b:
                project_layer0(b)
                layer_passes(b, 0)
                project_layer1(b)
                layer_passes(b, 1)

        @block.scalar
        def _(act):
            def exponentials(b, layer, g):
                n = tile0(b, layer, g)

                def tile(kt, c):
                    act.wait_ge(col_ready, n + kt * PER + c + 1)
                    act.wait_ge(exp_free, n + kt * PER + c + 1)
                    act.activation(w_exp[:, c, :], col_ps[:, c % 2, :], ACT.Exp,
                                   scale=logit[:, (0, 2)[layer]:(1, 3)[layer]]).then_inc(exp_ready, 1)

                with act.Fori(0, NK) as kt:
                    for c in range(PER):
                        tile(kt, c)
                if layer == 0:
                    for c in range(BC):
                        act.wait_ge(col_ready, n + NC + c + 1)
                        act.activation(w_bank[:, c, :], col_ps[:, c % 2, :], ACT.Exp,
                                       scale=logit[:, 1:2]).then_inc(exp_ready, 1)

            def max_rows(b, layer, g):
                act.wait_ge(max_psum_ready, group_no(b, layer, g) + 1)
                cols = bass.ds(g * GROUP, GROUP)
                if layer == 0:
                    act.activation(bank_max[:, :], max_ps[0:2, :], ACT.Copy)
                    act.activation(q0[S0:R0, cols], max_ps[S0:R0, :], ACT.Copy).then_inc(max_rows_ready, 1)
                else:
                    act.activation(q1b[C:R1, cols], max_ps[C:R1, :], ACT.Copy).then_inc(max_rows_ready, 1)

            def layer_passes(b, layer):
                max_rows(b, layer, 0)
                with act.Fori(0, NG - 1) as g:
                    exponentials(b, layer, g)
                    max_rows(b, layer, g + 1)
                exponentials(b, layer, NG - 1)

            with act.Fori(0, B) as b:
                act.wait_ge(scale0_ready, b + 1)
                for j in range(NK):
                    if j >= 2:
                        act.wait_ge(stack0_ready, b * NK + j - 1)
                    act.wait_ge(theta_psum_ready, b * NK + j + 1)
                    act.activation(full32[:, 0, j % 2, :], max_ps[0:S0, :], ACT.Identity,
                                   scale=scale[0:S0, 0:1], bias=b_scaled[0:S0, 0:1]).then_inc(theta_ready, 1)
                    act.wait_ge(phi_psum_ready, b * NK + j + 1)
                    act.activation(full32[:, 1, j % 2, :], yt_ps[0:S0, :], ACT.Identity,
                                   scale=scale[0:S0, 1:2], bias=b_scaled[0:S0, 1:2]).then_inc(phi_ready, 1)
                layer_passes(b, 0)
                act.wait_ge(scale1_ready, b + 1)
                with act.Fori(0, NK) as j:
                    cols = bass.ds(j * GROUP, GROUP)
                    act.activation(k1a[:, cols], x1[:, cols], ACT.Copy, scale=scale1[:, :]).then_inc(k1a_ready, 1)
                    act.wait_ge(v_psum_ready, (2 * b + 1) * NK + j + 1)
                    act.activation(v1[:, bass.ds(j * PER, PER), 0:C],
                                   proj_ps[:, 0:PER * C].rearrange("p (i c) -> p i c", c=C),
                                   ACT.Copy).then_inc(v1_ready, 1)
                layer_passes(b, 1)

        @block.gpsimd
        def _(pool):
            pool.wait_ge(stats_ready, 3)
            pool.partition_all_reduce(stat_all[:, :], stat[:, :], P, RMAX).then_inc(stats_all_ready, 1)
            with pool.Fori(0, B) as b:
                pool.wait_ge(peak_ready, 2 * b + 1)
                pool.sem_inc(peak_seen, 1)
                pool.partition_all_reduce(peak_all[:, :], peak[:, :], P, RMAX).then_inc(peak_all_ready, 1)
                pool.wait_ge(peak_ready, 2 * b + 2)
                pool.sem_inc(peak_seen, 1)
                pool.partition_all_reduce(peak_all[:, :], peak[:, :], P, RMAX).then_inc(peak_all_ready, 1)
                with pool.Fori(0, NK) as j:
                    cols = bass.ds(j * GROUP, GROUP)
                    pool.wait_ge(k1a_ready, b * NK + j + 1)
                    pool.tensor_copy(q1a[0:C, cols], k1a[0:C, cols])
                    pool.tensor_copy(q1b[0:C, cols], k1a[0:C, cols]).then_inc(hi1_ready, 1)

        @block.vector
        def _(v):
            def powers(peaks, n, width):
                bits = peaks.bitcast(U32)
                v.tensor_scalar(pow_dn[:, 0:width].bitcast(U32), bits, EXPONENT, None, ALU.bitwise_and)
                v.tensor_scalar(pow_up[:, 0:width].bitcast(U32), bits, EXPONENT, EXPONENT,
                                ALU.bitwise_xor, ALU.bitwise_and).then_inc(scale_step, 1)
                v.wait_ge(scale_step, n + 1)
                return n + 1

            def image_scales(b):
                n = b * 8 + 2
                v.tensor_reduce(peak[:, :], x_sb[:, :], AX_X, ALU.max, apply_absolute_value=True)\
                    .then_inc(peak_ready, 1)
                v.wait_ge(peak_all_ready, 2 * b + 1)
                v.scalar_tensor_tensor(bound[:, :], stat_all[:, 0:2], peak_all[:, 0:1], stat_all[:, 2:4],
                                       ALU.mult, ALU.add).then_inc(scale_step, 1)
                v.wait_ge(scale_step, n + 1)
                v.tensor_scalar(bound[:, :], bound[:, :], TINY, None, ALU.max).then_inc(scale_step, 1)
                v.wait_ge(scale_step, n + 2)
                powers(bound[:, :], n + 2, 2)
                v.tensor_scalar(inv[:, :], pow_dn[:, :], 0.125, None, ALU.mult)
                v.tensor_scalar(scale[:, :], pow_up[:, :], 4.0, None, ALU.mult).then_inc(scale_step, 1)
                v.wait_ge(scale_step, n + 4)
                v.tensor_tensor(b_scaled[:, :], b_col[:, :], scale[:, :], ALU.mult)
                v.scalar_tensor_tensor(logit[:, 1:2], inv[:, 1:2], BANK_SCALE, bank_s[:, 1:2],
                                       ALU.mult, ALU.mult)
                v.tensor_tensor(logit[:, 0:1], inv[:, 0:1], inv[:, 1:2], ALU.mult).then_inc(scale0_ready, 1)

            def x1_scale(b):
                n = b * 8 + 6
                v.wait_ge(x1_max_ready, (b + 1) * NG)
                v.tensor_reduce(peak[:, :], x1_max[:, :], AX_X, ALU.max).then_inc(peak_ready, 1)
                v.wait_ge(peak_all_ready, 2 * b + 2)
                v.tensor_scalar(bound[:, 0:1], peak_all[:, :], TINY, None, ALU.max).then_inc(scale_step, 1)
                v.wait_ge(scale_step, n + 1)
                powers(bound[:, 0:1], n + 1, 1)
                v.tensor_scalar(inv[:, 0:1], pow_dn[:, 0:1], 0.125, None, ALU.mult).then_inc(scale_step, 1)
                v.tensor_scalar(scale1[:, :], pow_up[:, 0:1], 4.0, None, ALU.mult).then_inc(scale_step, 1)
                v.wait_ge(scale_step, n + 4)
                v.tensor_tensor(logit[:, 2:3], inv[:, 0:1], inv[:, 0:1], ALU.mult).then_inc(scale1_ready, 1)

            def split_layer0(b):
                for j in range(NK):
                    cols = slice(j * GROUP, (j + 1) * GROUP)
                    v.wait_ge(theta_ready, b * NK + j + 1)
                    v.tensor_copy(q0[0:S0, cols], full32[:, 0, j % 2, :]).then_inc(hi_ready, 1)
                    v.wait_ge(phi_ready, b * NK + j + 1)
                    v.tensor_copy(k0[0:S0, cols], full32[:, 1, j % 2, :]).then_inc(hi_ready, 1)
                    v.wait_ge(v_psum_ready, 2 * b * NK + j + 1)
                    v.tensor_tensor(v0[:, j * PER:(j + 1) * PER, 0:I],
                                    proj_ps[:, 0:PER * I].rearrange("p (i c) -> p i c", c=I),
                                    g_bias[:, :, :], ALU.add).then_inc(v0_ready, 1)
                    v.wait_ge(hi_ready, 2 * (b * NK + j) + 2)
                    v.tensor_tensor(q0[I:2 * I, cols], full32[I:2 * I, 0, j % 2, :], q0[I:2 * I, cols],
                                    ALU.subtract)
                    v.tensor_tensor(k0[2 * I:S0, cols], full32[2 * I:S0, 1, j % 2, :], k0[2 * I:S0, cols],
                                    ALU.subtract).then_inc(stack0_ready, 1)

            def split_layer1(b):
                v.wait_ge(out_stored, b * NG * 16)
                v.memset(q1b[C:R1, :], 0.0)
                with v.Fori(0, NK) as j:
                    cols = bass.ds(j * GROUP, GROUP)
                    v.wait_ge(k1a_ready, b * NK + j + 1)
                    v.scalar_tensor_tensor(k1b[0:C, cols], x1[0:C, cols], scale1[0:C, :], k1a[0:C, cols],
                                           ALU.mult, ALU.subtract)
                    v.scalar_tensor_tensor(q1a[C:P, cols], x1[C:P, cols], scale1[C:P, :], k1a[C:P, cols],
                                           ALU.mult, ALU.subtract).then_inc(lo1_ready, 1)

            def row_maxima(b, layer, g):
                n = tile0(b, layer, g)
                with v.Fori(0, NK) as kt:
                    for i in range(PER):
                        v.wait_ge(row_ready, n + kt * PER + i + 1)
                        v.tensor_reduce(max_part[:, i, bass.ds(kt, 1)], row_ps[:, i % 2, :],
                                        AX_X, ALU.max).then_inc(row_free, 1)
                if layer == 0:
                    for t in range(BC):
                        v.wait_ge(row_ready, n + NC + t + 1)
                        v.tensor_reduce(neg_max[:, PER + 2 * t:PER + 2 * t + 2],
                                        row_ps[:, t, :].rearrange("p (i k) -> p i k", k=BANK),
                                        AX_X, ALU.max, negate=True).then_inc(row_free, 1)

            def group_maxima(b, layer, g):
                n = group_no(b, layer, g)
                wide = (2 * PER, PER)[layer]
                v.wait_ge(row_free, tile0(b, layer, g) + T[layer] + 2)
                v.tensor_reduce(neg_max[:, 0:PER], max_part[:, :, :], AX_X, ALU.max, negate=True)\
                    .then_inc(neg_max_ready, 1)
                v.wait_ge(neg_max_ready, n + 1)
                v.tensor_copy(max_cols[:, 0:wide, 0], neg_max[:, 0:wide]).then_inc(max_hi_ready, 1)
                v.wait_ge(max_hi_ready, n + 1)
                v.tensor_tensor(max_cols[:, 0:wide, 1], neg_max[:, 0:wide], max_cols[:, 0:wide, 0],
                                ALU.subtract).then_inc(max_cols_ready, 1)

            def normalise(b, layer, g):
                n = group_no(b, layer, g)
                lanes, w = LANES[layer], WIDE[layer]
                sums = acc_ps[:, 0:lanes * w].rearrange("p (s w) -> p s w", w=w)
                v.wait_ge(exp_free, tile0(b, layer, g) + T[layer] + PER)
                v.reciprocal(recip[:, 0:lanes], sums[:, :, w - 1]).then_inc(recip_ready, 1)
                v.wait_ge(recip_ready, n + 1)
                rows = y_norm[:, :, :] if layer else \
                    y_norm[:, :, :].rearrange("p q (r c) -> p r q c", c=I)
                if layer:
                    v.tensor_tensor(rows, sums[:, :, 0:w - 1],
                                    recip[:, 0:lanes].unsqueeze(2).broadcast_to([P, lanes, w - 1]),
                                    ALU.mult).then_inc(y_ready, 1)
                else:
                    v.tensor_tensor(rows, sums[:, :, 0:w - 1].rearrange("p (r q) c -> p r q c", q=PER),
                                    recip[:, :].rearrange("p (r q) -> p r q", q=PER).unsqueeze(3)
                                    .broadcast_to([P, BC, PER, w - 1]), ALU.mult).then_inc(y_ready, 1)

            def group_out(b, layer, g):
                n = group_no(b, layer, g)
                cols = bass.ds(g * GROUP, GROUP)
                v.wait_ge(yt_psum_ready, n + 1)
                if layer == 0:
                    v.tensor_copy(y_t[:, :], yt_ps[0:C, :]).then_inc(yt_done, 1)
                    v.wait_ge(proj_psum_ready, b * NG + g + 1)
                    v.scalar_tensor_tensor(x1[:, cols], proj_ps[:, :], b_out[:, :], x_sb[:, cols],
                                           ALU.add, ALU.add).then_inc(x1_ready, 1)
                    v.wait_ge(x1_ready, b * NG + g + 1)
                    v.tensor_reduce(x1_max[:, bass.ds(g, 1)], x1[:, cols], AX_X, ALU.max,
                                    apply_absolute_value=True).then_inc(x1_max_ready, 1)
                else:
                    v.tensor_tensor(out_sb[:, cols], yt_ps[0:C, :], x1[0:C, cols], ALU.add)\
                        .then_inc(yt_done, 1)

            def layer_passes(b, layer):
                row_maxima(b, layer, 0)
                group_maxima(b, layer, 0)
                with v.Fori(0, NG - 1) as g:
                    row_maxima(b, layer, g + 1)
                    group_maxima(b, layer, g + 1)
                    normalise(b, layer, g)
                    group_out(b, layer, g)
                normalise(b, layer, NG - 1)
                group_out(b, layer, NG - 1)

            v.memset(ones2[:, :], 1.0).then_inc(consts_set, 1)
            v.memset(zero16[:, :], 0.0).then_inc(consts_set, 1)
            v.memset(k0[S0:R0, :], 1.0).then_inc(consts_set, 1)
            v.memset(k1b[C:R1, :], 1.0).then_inc(consts_set, 1)
            v.memset(v0[:, :, I:I + 1], 1.0).then_inc(consts_set, 1)
            v.memset(v1[:, :, C:C + 1], 1.0).then_inc(consts_set, 1)
            v.memset(bank_val[:, :, I:I + 1], 1.0).then_inc(consts_set, 1)
            v.memset(recip[:, :], 1.0).then_inc(row_free, 2)
            v.memset(y_norm[:, :, :], 0.0).then_inc(exp_free, PER)
            v.wait_ge(weights_loaded, len(WEIGHT_LOADS) * 16)
            v.tensor_copy(ident16[:, :], ident[:, :]).then_inc(consts_set, 1)
            v.tensor_tensor(b_out[:, :], b_out2[:, 0:1], b_out2[:, 1:2], ALU.add).then_inc(consts_set, 1)
            v.tensor_reduce(stat[:, 0:2], w_stat[:, :, :], AX_X, ALU.add, apply_absolute_value=True)\
                .then_inc(stats_ready, 1)
            v.tensor_reduce(stat[:, 2:4], b_col[:, :].unsqueeze(2), AX_X, ALU.max,
                            apply_absolute_value=True).then_inc(stats_ready, 1)
            v.tensor_reduce(stat[:, 4:5], bank[:, :], AX_X, ALU.max, apply_absolute_value=True)\
                .then_inc(stats_ready, 1)
            v.wait_ge(stats_all_ready, 1)
            v.tensor_scalar(bound[:, 0:1], stat_all[:, 4:5], TINY, None, ALU.max).then_inc(scale_step, 1)
            v.wait_ge(scale_step, 1)
            powers(bound[:, 0:1], 1, 1)
            v.tensor_scalar(bank_s[:, 0:1], pow_up[:, 0:1], 4.0, None, ALU.mult).then_inc(consts_set, 1)
            v.tensor_scalar(bank_s[:, 1:2], pow_dn[:, 0:1], 0.125, None, ALU.mult).then_inc(consts_set, 1)
            v.wait_ge(consts_set, 11)
            v.tensor_scalar(bank32[:, :], bank[:, :], bank_s[:, 0:1], None, ALU.mult).then_inc(bank_step, 1)
            v.wait_ge(bank_step, 1)
            v.tensor_copy(bank_stack[:, :], bank32[:, :]).then_inc(bank_step, 1)
            v.wait_ge(bank_step, 2)
            v.tensor_tensor(bank_stack[I:2 * I, :], bank32[I:2 * I, :], bank_stack[I:2 * I, :],
                            ALU.subtract).then_inc(bank_step, 2)
            with v.Fori(0, B) as b:
                v.wait_ge(x_loaded, (b + 1) * 32)
                image_scales(b)
                split_layer0(b)
                layer_passes(b, 0)
                x1_scale(b)
                split_layer1(b)
                layer_passes(b, 1)


def kernel(x, L0_conv_g_w, L0_conv_g_b, L0_conv_theta_w, L0_conv_theta_b, L0_conv_phi_w, L0_conv_phi_b,
           L0_conv_W_w, L0_conv_W_b, L0_conv_Wz1_w, L0_conv_Wz1_b, L0_conv_mb, L1_conv_weight):
    import numpy as np
    import concourse.bacc as bacc
    from concourse.bass_utils import run_bass_kernel_spmd

    def a(t):
        return np.asarray(t)

    nb, c, h, w = x.shape
    inter = L0_conv_g_w.shape[0]
    chunks = L0_conv_mb.shape[1] // P
    theta_t, phi_t = a(L0_conv_theta_w).T, a(L0_conv_phi_w).T
    arrays = {
        "x": np.ascontiguousarray(a(x).reshape(nb, c, h * w)),
        "weights": np.ascontiguousarray(np.concatenate(
            [theta_t] * 3 + [phi_t] * 3 + [a(L0_conv_g_w).T, a(L1_conv_weight)], axis=1)),
        "wstat": np.ascontiguousarray(np.stack(
            [np.tile(a(L0_conv_theta_w), (P // inter, 1)), np.tile(a(L0_conv_phi_w), (P // inter, 1))], axis=1)),
        "bcol": np.ascontiguousarray(np.stack(
            [np.tile(a(L0_conv_theta_b), P // inter), np.tile(a(L0_conv_phi_b), P // inter)], axis=1)),
        "out_w": np.ascontiguousarray(np.concatenate(
            [np.tile(a(L0_conv_W_w).T, (1, 2)), np.tile(a(L0_conv_Wz1_w).T, (1, 2))], axis=0)),
        "out_b": np.ascontiguousarray(np.stack(
            [np.tile(a(L0_conv_W_b), 2), np.tile(a(L0_conv_Wz1_b), 2)], axis=1)),
        "g_bias": np.ascontiguousarray(np.broadcast_to(a(L0_conv_g_b), (P, GROUP // P, inter))),
        "bank": np.ascontiguousarray(np.tile(a(L0_conv_mb), (P // inter, 1))),
        "bank_t": np.ascontiguousarray(a(L0_conv_mb).T.reshape(chunks, P, inter).transpose(1, 0, 2)),
        "ident": np.eye(P, dtype=np.float32),
    }
    nc = bacc.Bacc("TRN2", target_bir_lowering=False, num_devices=1)
    args = [nc.dram_tensor(f"{name}_dram", t.shape, mybir.dt.from_np(t.dtype), kind="ExternalInput").ap()
            for name, t in arrays.items()]
    out = nc.dram_tensor("out_dram", arrays["x"].shape, F32, kind="ExternalOutput").ap()
    non_local_then_graph(nc, *args, out)
    r = run_bass_kernel_spmd(nc, [{f"{name}_dram": t for name, t in arrays.items()}], core_ids=[0])
    return r.results[0]["out_dram"].reshape(nb, c, h, w)
```

```python
from contextlib import ExitStack

import concourse.bass as bass
from concourse import mybir

ALU = mybir.AluOpType
ACT = mybir.ActivationFunctionType
AX_X = mybir.AxisListType.X
F32 = mybir.dt.float32
F16 = mybir.dt.float16
BF16 = mybir.dt.bfloat16
U32 = mybir.dt.uint32
RMAX = bass.bass_isa.ReduceOp.max

P = 128
GROUP = 512
EXPONENT = 0x7F800000
TINY = 1e-30
LIFT = 8 * 0.6931471805599453
LIFT_MOST = 16000.0


def non_local_then_graph(nc, x, weights_in, wstat_in, bstat_in, out_w_in, out_b_in, g_bias_in,
                         bank_in, bank_t_in, ident_in, out):
    B, C, N = x.shape
    I = C // 2
    NG = N // GROUP
    NK = N // GROUP
    NC = N // P
    PER = GROUP // P
    BANK = bank_in.shape[1]
    BC = BANK // P
    S0 = 3 * I
    R0 = S0 + 2
    R1 = C + 2
    MAIN = [2 * I + 1, C + 1]
    BANKW = I + 1
    ACC = [PER * (MAIN[0] + BANKW), PER * MAIN[1]]
    T = [NC + BC, NC]
    PER_IMAGE = NG * (T[0] + T[1])
    BANK_SCALE = float(I) ** -0.5
    POOL_COLS = 320
    WCOLS = [(0, S0), (S0, 2 * S0), (2 * S0, 2 * S0 + I), (2 * S0 + I, 2 * S0 + I + C)]
    assert S0 <= 96 and NC == 32 and BC == 2 and PER == 4

    SPLITS = [(2 * NK + 1, 3 * NK + 1), (2 * NK, 2 * NK)]

    def tile0(b, layer, g):
        return b * PER_IMAGE + (NG * T[0] if layer else 0) + g * T[layer]

    def group_no(b, layer, g):
        return b * (2 * NG) + layer * NG + g

    def splits0(who, b, layer, g):
        per_image = NG * (SPLITS[0][who] + SPLITS[1][who])
        return b * per_image + (NG * SPLITS[0][who] if layer else 0) + g * SPLITS[layer][who]

    with ExitStack() as ctx:
        def sb(name, shape, dt):
            return ctx.enter_context(nc.sbuf_tensor(name, shape, dt))

        def psum(name, shape, dt):
            return ctx.enter_context(nc.psum_tensor(name, shape, dt))

        def sem(name):
            return ctx.enter_context(nc.semaphore(name))

        WALL = WCOLS[-1][1]
        w_proj = sb("w_proj", [P, WALL], F32)
        w_scaled = sb("w_scaled", [P, WALL], F32)
        w16 = sb("w16", [P, 2, WALL], F16)
        w_stat = sb("w_stat", [P, 6, C], F32)
        b_stat = sb("b_stat", [P, 5], F32)
        w_out = sb("w_out", [C, 2 * C], F32)
        b_out2 = sb("b_out2", [P, 2], F32)
        b_out = sb("b_out", [P, 1], F32)
        g_bias = sb("g_bias", [P, PER * I], F32)
        bank = sb("bank", [P, BANK], F32)
        bank_t = sb("bank_t", [P, BC, I], F32)
        bank_val = sb("bank_val", [P, BC, 2 * I + 1], F16)
        ident = sb("ident", [P, P], F32)
        ident16 = sb("ident16", [P, P], F16)
        ones2 = sb("ones2", [C + 2, P], F16)
        zero16 = sb("zero16", [32, GROUP], F16)
        x_sb = sb("x_sb", [P, N], F32)
        x16 = sb("x16", [P, N], F16)
        full32 = sb("full32", [S0, 2, GROUP], F32)
        q0 = sb("q0", [P, N], F16)
        k0 = sb("k0", [P, N], F16)
        bank32 = sb("bank32", [P, BANK], F32)
        bank_stack = sb("bank_stack", [P, BANK], F16)
        v0 = sb("v0", [P, NC, 2 * I + 1], F16)
        v32 = sb("v32", [P, PER * C], F32)
        x1 = sb("x1", [P, N], F32)
        x1_full = sb("x1_full", [P, 2, GROUP], F32)
        q1a = sb("q1a", [P, N], F16)
        k1a = sb("k1a", [P, N], F16)
        q1b = sb("q1b", [P, N], F16)
        k1b = sb("k1b", [P, N], F16)
        v1 = sb("v1", [P, NC, 2 * C + 1], F16)
        out_sb = sb("out_sb", [C, N], F32)
        w_exp = sb("w_exp", [P, PER, GROUP], F32)
        w_rest = sb("w_rest", [P, PER, GROUP], F16)
        e_bank = sb("e_bank", [P, BC, GROUP], F32)
        e_bank_rest = sb("e_bank_rest", [P, BC, GROUP], F16)
        bank_max = sb("bank_max", [C + 2, GROUP], F16)
        max_part = sb("max_part", [P, PER, NK], F32)
        neg_max = sb("neg_max", [P, 2 * PER], F32)
        max_cols = sb("max_cols", [P, 2 * PER, 2], F16)
        acc_sb = sb("acc_sb", [P, ACC[0]], F32)
        recip = sb("recip", [P, 2 * PER], F32)
        y_sum = sb("y_sum", [P, PER * I], F32)
        y_norm = sb("y_norm", [P, PER, C], F32)
        y_t = sb("y_t", [C, GROUP], F32)
        NSTAT = 6 + 5 + 4 + 1
        stat = sb("stat", [P, NSTAT], F32)
        stat_all = sb("stat_all", [P, NSTAT], F32)
        peak = sb("peak", [P, 1], F32)
        peak_all = sb("peak_all", [P, 1], F32)
        out_const = sb("out_const", [P, 1], F32)
        bound = sb("bound", [P, 6], F32)
        w_clamp = sb("w_clamp", [P, 5], F32)
        pow_up = sb("pow_up", [P, 6], F32)
        pow_dn = sb("pow_dn", [P, 6], F32)
        w_s = sb("w_s", [P, 5], F32)
        w_i = sb("w_i", [P, 5], F32)
        scale0 = sb("scale0", [P, 4], F32)
        inv0 = sb("inv0", [P, 4], F32)
        scale1 = sb("scale1", [P, 2], F32)
        inv1 = sb("inv1", [P, 2], F32)
        factor = sb("factor", [P, 4], F32)
        b_scaled = sb("b_scaled", [P, 2], F32)
        g_bias_scaled = sb("g_bias_scaled", [P, PER * I], F32)
        logit = sb("logit", [P, 3], F32)
        lift = sb("lift", [P, 3], F32)

        row_ps = psum("row_ps", [P, 2, GROUP], F32)
        col_ps = psum("col_ps", [P, 2, GROUP], F32)
        acc_ps = psum("acc_ps", [P, GROUP], F32)
        turn_ps = psum("turn_ps", [P, GROUP], F32)
        proj_ps = psum("proj_ps", [P, GROUP], F32)
        phi_ps = psum("phi_ps", [P, GROUP], F32)

        weights_loaded = sem("weights_loaded")
        x_loaded = sem("x_loaded")
        out_stored = sem("out_stored")
        consts_set = sem("consts_set")
        stats_ready = sem("stats_ready")
        stats_all_ready = sem("stats_all_ready")
        setup_step = sem("setup_step")
        peak_ready = sem("peak_ready")
        peak_seen = sem("peak_seen")
        peak_all_ready = sem("peak_all_ready")
        scale_step = sem("scale_step")
        scale0_ready = sem("scale0_ready")
        scale1_ready = sem("scale1_ready")
        x_hi_ready = sem("x_hi_ready")
        x16_ready = sem("x16_ready")
        theta_psum_ready = sem("theta_psum_ready")
        phi_psum_ready = sem("phi_psum_ready")
        v_psum_ready = sem("v_psum_ready")
        theta_ready = sem("theta_ready")
        phi_ready = sem("phi_ready")
        v32_ready = sem("v32_ready")
        v_hi_ready = sem("v_hi_ready")
        v_ready = sem("v_ready")
        stack0_ready = sem("stack0_ready")
        x1_hi_ready = sem("x1_hi_ready")
        x1_lo_ready = sem("x1_lo_ready")
        row_ready = sem("row_ready")
        row_free = sem("row_free")
        col_ready = sem("col_ready")
        exp_ready = sem("exp_ready")
        exp_free = sem("exp_free")
        split_v = sem("split_v")
        split_p = sem("split_p")
        neg_max_ready = sem("neg_max_ready")
        max_hi_ready = sem("max_hi_ready")
        max_cols_ready = sem("max_cols_ready")
        max_psum_ready = sem("max_psum_ready")
        max_rows_ready = sem("max_rows_ready")
        acc_free = sem("acc_free")
        norm_step = sem("norm_step")
        y_ready = sem("y_ready")
        y_seen = sem("y_seen")
        yt_psum_ready = sem("yt_psum_ready")
        yt_free = sem("yt_free")
        proj_psum_ready = sem("proj_psum_ready")
        x1_ready = sem("x1_ready")

        WEIGHT_LOADS = [
            (w_proj[:, :], weights_in[:, :]), (w_stat[:, :, :], wstat_in[:, :, :]),
            (b_stat[:, :], bstat_in[:, :]), (w_out[:, :], out_w_in[:, :]),
            (b_out2[:, :], out_b_in[:, :]), (g_bias[:, :], g_bias_in[:, :]),
            (bank[:, :], bank_in[:, :]), (bank_t[:, :, :], bank_t_in[:, :, :]),
            (ident[:, :], ident_in[:, :]),
        ]
        WEIGHTS_IN = len(WEIGHT_LOADS) * 16
        CONSTS, SETUP = 12, 9

        exp_upper = w_exp[:, :, :].bitcast(BF16)
        bank_upper = e_bank[:, :, :].bitcast(BF16)

        def upper(view, slot, first, count):
            return view[:, slot, 2 * first + 1:2 * (first + count):2]

        block = ctx.enter_context(nc.Block())

        @block.sync
        def _(sp):
            def load_image(b):
                for half in range(2):
                    sp.dma_start(x_sb[half * C:(half + 1) * C, :],
                                 x[bass.ds(b, 1)].rearrange("a c n -> (a c) n")).then_inc(x_loaded, 16)

            def store_group(b, g):
                sp.wait_ge(yt_free, group_no(b, 1, g) + 2)
                sp.dma_start(out[bass.ds(b, 1), :, bass.ds(g * GROUP, GROUP)].rearrange("a c n -> (a c) n"),
                             out_sb[:, bass.ds(g * GROUP, GROUP)]).then_inc(out_stored, 16)

            load_image(0)
            for dst, src in WEIGHT_LOADS:
                sp.dma_start(dst, src).then_inc(weights_loaded, 16)
            with sp.Fori(0, B - 1) as b:
                sp.wait_ge(x1_ready, (b + 1) * NG + 1)
                load_image(b + 1)
                with sp.Fori(0, NG) as g:
                    store_group(b, g)
            with sp.Fori(0, NG) as g:
                store_group(B - 1, g)
            sp.wait_ge(out_stored, B * NG * 16)

        @block.tensor
        def _(pe):
            def row_tile(b, layer, g, kt, i):
                pe.wait_ge(row_free, tile0(b, layer, g) + kt * PER + i + 1)
                queries = bass.ds(g * GROUP + i * P, P)
                keys = bass.ds(kt * GROUP, GROUP)
                if layer == 0:
                    mm = pe.matmul(row_ps[:, i % 2, :], q0[0:S0, queries], k0[0:S0, keys],
                                   start=True, stop=True)
                else:
                    pe.matmul(row_ps[:, i % 2, :], q1a[:, queries], k1a[:, keys], start=True, stop=False)
                    mm = pe.matmul(row_ps[:, i % 2, :], q1b[0:R1, queries], k1b[0:R1, keys],
                                   start=False, stop=True)
                mm.then_inc(row_ready, 1)

            def row_bank(b, g, t):
                pe.wait_ge(row_free, tile0(b, 0, g) + NC + t + 1)
                for i in range(2):
                    mm = pe.matmul(row_ps[:, t, i * BANK:(i + 1) * BANK],
                                   k0[0:S0, bass.ds(g * GROUP + (2 * t + i) * P, P)],
                                   bank_stack[0:S0, :], start=True, stop=True)
                mm.then_inc(row_ready, 1)

            def col_tile(layer, g, kt, c):
                keys = bass.ds(kt * GROUP + c * P, P)
                queries = bass.ds(g * GROUP, GROUP)
                if layer == 0:
                    mm = pe.matmul(col_ps[:, c % 2, :], k0[0:R0, keys], q0[0:R0, queries],
                                   start=True, stop=True)
                else:
                    pe.matmul(col_ps[:, c % 2, :], k1a[:, keys], q1a[:, queries], start=True, stop=False)
                    mm = pe.matmul(col_ps[:, c % 2, :], k1b[0:R1, keys], q1b[0:R1, queries],
                                   start=False, stop=True)
                mm.then_inc(col_ready, 1)

            def col_bank(g, c):
                pe.matmul(col_ps[:, c % 2, :], bank_stack[0:S0, c * P:(c + 1) * P],
                          k0[0:S0, bass.ds(g * GROUP, GROUP)], start=True, stop=False)
                pe.matmul(col_ps[:, c % 2, :], ones2[C:C + 2, :], bank_max[C:C + 2, :],
                          start=False, stop=True).then_inc(col_ready, 1)

            def weigh(b, layer, g, kt, c, last):
                done_v, done_p = splits0(0, b, layer, g), splits0(1, b, layer, g)
                if layer == 0:
                    if c % 2 == 0:
                        pe.wait_ge(split_p, done_p + 3 * kt + c // 2 + 1)
                    elif c == 1:
                        pe.wait_ge(split_v, done_v + 2 * kt + 1)
                    else:
                        pe.wait_ge(split_v, done_v + 2 * kt + 2)
                        pe.wait_ge(split_p, done_p + 3 * kt + 3)
                elif c % 2 == 0:
                    pe.wait_ge(split_p, done_p + 2 * kt + c // 2 + 1)
                else:
                    pe.wait_ge(split_v, done_v + 2 * kt + c // 2 + 1)
                w = MAIN[layer]
                chunk = bass.ds(kt * PER + c, 1)
                for i in range(PER):
                    for part in (upper(exp_upper, c, i * P, P), w_rest[:, c, i * P:(i + 1) * P]):
                        if layer == 0:
                            mm = pe.matmul(acc_ps[:, i * w:(i + 1) * w], part,
                                           v0[:, chunk, :].rearrange("p a w -> p (a w)"),
                                           start=False, stop=last, skip_group_check=True)
                        else:
                            pe.matmul(acc_ps[:, i * w:(i + 1) * w], part,
                                      v1[:, chunk, 0:C + 1].rearrange("p a w -> p (a w)"),
                                      start=False, stop=last, skip_group_check=True)
                            mm = pe.matmul(acc_ps[:, i * w:i * w + C], part,
                                           v1[:, chunk, C + 1:].rearrange("p a w -> p (a w)"),
                                           start=False, stop=last, skip_group_check=True)
                mm.then_inc(exp_free, 1)

            def weigh_bank(b, g, c):
                if c == 0:
                    pe.wait_ge(split_p, splits0(1, b, 0, g + 1))
                else:
                    pe.wait_ge(split_v, splits0(0, b, 0, g + 1))
                for i in range(PER):
                    at = PER * MAIN[0] + i * BANKW
                    for part in (upper(bank_upper, c, i * P, P), e_bank_rest[:, c, i * P:(i + 1) * P]):
                        pe.matmul(acc_ps[:, at:at + BANKW], part, bank_val[:, c, 0:BANKW],
                                  start=False, stop=c == BC - 1, skip_group_check=True)
                        mm = pe.matmul(acc_ps[:, at:at + I], part, bank_val[:, c, BANKW:],
                                       start=False, stop=c == BC - 1, skip_group_check=True)
                mm.then_inc(exp_free, 1)

            def turn_maxima(b, layer, g):
                pe.wait_ge(max_cols_ready, group_no(b, layer, g) + 1)
                row = (S0, C)[layer]
                for i in range(PER):
                    mm = pe.matmul(turn_ps[row:row + 2, i * P:(i + 1) * P], max_cols[:, i, :], ident16[:, :],
                                   start=True, stop=True, skip_group_check=True)
                if layer == 0:
                    for i in range(PER):
                        mm = pe.matmul(turn_ps[C:C + 2, i * P:(i + 1) * P], max_cols[:, PER + i, :],
                                       ident16[:, :], start=True, stop=True, skip_group_check=True)
                mm.then_inc(max_psum_ready, 1)

            def step(b, layer, g, kt, c, nxt, first=False):
                if nxt:
                    row_tile(b, layer, g + 1, kt + 1, c)
                pe.wait_ge(exp_ready, tile0(b, layer, g) + kt * PER + c + 2)
                col_tile(layer, g, kt, c + 3)
                if first:
                    pe.wait_ge(acc_free, group_no(b, layer, g) + 1)
                    pe.matmul(acc_ps[:, 0:ACC[layer]], zero16[:, 0:P], zero16[:, 0:ACC[layer]],
                              start=True, stop=False, skip_group_check=True)
                weigh(b, layer, g, kt, c, False)

            def steps(b, layer, g, kt, nxt, first=False):
                for c in range(PER):
                    step(b, layer, g, kt, c, nxt, first and c == 0)

            def last_steps(b, layer, g, nxt, nxt2):
                n = tile0(b, layer, g)
                kt = NK - 1
                rows_from = T[layer] - PER
                for s in range(kt * PER, T[layer]):
                    if s < rows_from and nxt:
                        row_bank(b, g + 1, s - kt * PER)
                    if s >= rows_from and nxt2:
                        row_tile(b, layer, g + 2, 0, s - rows_from)
                    ahead = s + 3
                    if ahead < T[layer] or nxt:
                        pe.wait_ge(exp_ready, n + s + 2)
                    if ahead < NC:
                        col_tile(layer, g, kt, ahead - kt * PER)
                    elif ahead < T[layer]:
                        col_bank(g, ahead - NC)
                    elif nxt:
                        if ahead == T[layer]:
                            pe.wait_ge(max_rows_ready, group_no(b, layer, g + 1) + 1)
                        col_tile(layer, g + 1, 0, ahead - T[layer])
                    if s < NC:
                        weigh(b, layer, g, kt, s - kt * PER, s == NC - 1)
                    else:
                        weigh_bank(b, g, s - NC)
                    if nxt and s == rows_from:
                        turn_maxima(b, layer, g + 1)

            def turn_rows(b, layer, g):
                n = group_no(b, layer, g)
                pe.wait_ge(yt_free, n + 1)
                pe.wait_ge(y_ready, n + 2)
                pe.sem_inc(y_seen, 1)
                for i in range(PER):
                    mm = pe.transpose(turn_ps[0:C, i * P:(i + 1) * P], y_norm[:, i, :], ident[:, :])
                mm.then_inc(yt_psum_ready, 1)

            def project_out(b, g):
                pe.wait_ge(yt_free, group_no(b, 0, g) + 2)
                pe.wait_ge(x1_ready, b * NG + g + 1)
                pe.matmul(proj_ps[:, :], w_out[:, :], y_t[:, :], start=True, stop=True)\
                    .then_inc(proj_psum_ready, 1)

            def head(b, layer, g, nxt, finish):
                steps(b, layer, g, 0, nxt, first=True)
                steps(b, layer, g, 1, nxt)
                if finish:
                    turn_rows(b, layer, g - 1)
                if layer == 0:
                    steps(b, layer, g, 2, nxt)
                    if finish:
                        project_out(b, g - 1)
                    steps(b, layer, g, 3, nxt)
                else:
                    with pe.Fori(2, 4) as kt:
                        steps(b, layer, g, kt, nxt)

            def rest(b, layer, g, nxt, nxt2):
                with pe.Fori(4, NK - 1) as kt:
                    steps(b, layer, g, kt, nxt)
                last_steps(b, layer, g, nxt, nxt2)

            def project_image(j):
                cols = bass.ds(j * GROUP, GROUP)
                for ps, (c0, c1), done in ((proj_ps, WCOLS[0], theta_psum_ready),
                                           (phi_ps, WCOLS[1], phi_psum_ready)):
                    pe.matmul(ps[0:S0, :], w16[:, 0, c0:c1], x16[:, cols], start=True, stop=False)
                    pe.matmul(ps[0:S0, :], w16[:, 1, c0:c1], x16[:, cols], start=False, stop=True)\
                        .then_inc(done, 1)

            def project_values(stack, which, j, ps):
                c0, c1 = WCOLS[which]
                w = c1 - c0
                for i in range(PER):
                    tokens = bass.ds(j * GROUP + i * P, P)
                    pe.matmul(ps[:, i * w:(i + 1) * w], stack[:, tokens], w16[:, 0, c0:c1],
                              start=True, stop=False)
                    mm = pe.matmul(ps[:, i * w:(i + 1) * w], stack[:, tokens], w16[:, 1, c0:c1],
                                   start=False, stop=True)
                mm.then_inc(v_psum_ready, 1)

            def row_tiles(b, layer, g, kt):
                for i in range(PER):
                    row_tile(b, layer, g, kt, i)

            def fill0(b):
                def tile(j, rows):
                    pe.wait_ge(x16_ready, b * NK + j + 1)
                    pe.wait_ge(v_ready, 2 * b * NK + j + 1)
                    project_image(j)
                    if rows:
                        pe.wait_ge(stack0_ready, b * NK + j + 1)
                        row_tiles(b, 0, 0, j - 1)
                    pe.wait_ge(phi_ready, b * NK + j + 1)
                    project_values(x16, 2, j, proj_ps)

                tile(0, False)
                with pe.Fori(1, NK) as j:
                    tile(j, True)
                pe.wait_ge(stack0_ready, (b + 1) * NK + 1)
                row_tiles(b, 0, 0, NK - 1)
                for t in range(BC):
                    row_bank(b, 0, t)
                row_tiles(b, 0, 1, 0)
                pe.wait_ge(v_ready, (2 * b + 1) * NK + 1)

            def fill1(b):
                def tile(j, rows):
                    pe.wait_ge(x1_lo_ready, b * NK + j + 2)
                    pe.wait_ge(v_ready, (2 * b + 1) * NK + j + 1)
                    project_values(q1a, 3, j, proj_ps)
                    if rows:
                        row_tiles(b, 1, 0, j - 1)

                tile(0, False)
                with pe.Fori(1, NK) as j:
                    tile(j, True)
                row_tiles(b, 1, 0, NK - 1)
                row_tiles(b, 1, 1, 0)
                pe.wait_ge(v_ready, 2 * (b + 1) * NK + 1)

            def passes(b, layer):
                turn_maxima(b, layer, 0)
                pe.wait_ge(max_rows_ready, group_no(b, layer, 0) + 1)
                for c in range(2):
                    col_tile(layer, 0, 0, c)
                pe.wait_ge(exp_ready, tile0(b, layer, 0) + 1)
                col_tile(layer, 0, 0, 2)
                head(b, layer, 0, True, False)
                with pe.Fori(0, NG - 2) as g:
                    rest(b, layer, g, True, True)
                    head(b, layer, g + 1, True, True)
                rest(b, layer, NG - 2, True, False)
                head(b, layer, NG - 1, False, True)
                rest(b, layer, NG - 1, False, False)
                turn_rows(b, layer, NG - 1)
                if layer == 0:
                    project_out(b, NG - 1)

            pe.wait_ge(weights_loaded, WEIGHTS_IN)
            pe.wait_ge(consts_set, CONSTS)
            pe.wait_ge(setup_step, SETUP)
            with pe.Fori(0, B) as b:
                fill0(b)
                passes(b, 0)
                fill1(b)
                passes(b, 1)

        @block.scalar
        def _(act):
            def exp_tile(b, layer, g, kt, c):
                n = tile0(b, layer, g) + kt * PER + c + 1
                act.wait_ge(col_ready, n)
                act.wait_ge(exp_free, n)
                lo = (0, 2)[layer]
                act.activation(w_exp[:, c % PER, :], col_ps[:, c % 2, :], ACT.Exp,
                               scale=logit[:, lo:lo + 1]).then_inc(exp_ready, 1)

            def exp_bank(b, g, c):
                n = tile0(b, 0, g) + NC + c + 1
                act.wait_ge(col_ready, n)
                act.wait_ge(exp_free, n)
                act.activation(e_bank[:, c, :], col_ps[:, c % 2, :], ACT.Exp,
                               scale=logit[:, 1:2]).then_inc(exp_ready, 1)

            def max_rows(b, layer, g):
                act.wait_ge(max_psum_ready, group_no(b, layer, g) + 1)
                cols = bass.ds(g * GROUP, GROUP)
                if layer == 0:
                    act.activation(bank_max[C:C + 2, :], turn_ps[C:C + 2, :], ACT.Copy)
                    act.activation(q0[S0:R0, cols], turn_ps[S0:R0, :], ACT.Copy).then_inc(max_rows_ready, 1)
                else:
                    act.activation(q1b[C:R1, cols], turn_ps[C:R1, :], ACT.Copy).then_inc(max_rows_ready, 1)

            def group(b, layer, g, nxt):
                with act.Fori(0, NK - 1) as kt:
                    for c in range(2, PER + 2):
                        exp_tile(b, layer, g, kt, c)
                exp_tile(b, layer, g, NK - 1, 2)
                if layer == 0:
                    exp_tile(b, layer, g, NK - 1, 3)
                    exp_bank(b, g, 0)
                if nxt:
                    max_rows(b, layer, g + 1)
                if layer == 0:
                    exp_bank(b, g, 1)
                else:
                    exp_tile(b, layer, g, NK - 1, 3)
                if nxt:
                    exp_tile(b, layer, g + 1, 0, 0)
                    exp_tile(b, layer, g + 1, 0, 1)
                act.wait_ge(exp_free, tile0(b, layer, g) + T[layer] + PER)
                act.wait_ge(y_ready, group_no(b, layer, g) + 1)
                act.activation(acc_sb[:, 0:ACC[layer]], acc_ps[:, 0:ACC[layer]], ACT.Copy)\
                    .then_inc(acc_free, 1)

            def passes(b, layer):
                max_rows(b, layer, 0)
                exp_tile(b, layer, 0, 0, 0)
                exp_tile(b, layer, 0, 0, 1)
                with act.Fori(0, NG - 1) as g:
                    group(b, layer, g, True)
                group(b, layer, NG - 1, False)

            with act.Fori(0, B) as b:
                act.wait_ge(scale0_ready, b + 1)
                with act.Fori(0, NK) as j:
                    cols = bass.ds(j * GROUP, GROUP)
                    act.activation(x16[:, cols], x_sb[:, cols], ACT.Copy, scale=scale0[:, 3:4])\
                        .then_inc(x_hi_ready, 1)
                    for n, (ps, stack, come, done) in enumerate(
                            ((proj_ps, q0, theta_psum_ready, theta_ready),
                             (phi_ps, k0, phi_psum_ready, phi_ready))):
                        act.wait_ge(come, b * NK + j + 1)
                        if n == 0:
                            act.wait_ge(stack0_ready, b * NK + j + 1)
                        act.activation(full32[:, n, :], ps[0:S0, :], ACT.Identity,
                                       scale=factor[0:S0, n:n + 1], bias=b_scaled[0:S0, n:n + 1])
                        act.activation(stack[0:S0, cols], ps[0:S0, :], ACT.Identity,
                                       scale=factor[0:S0, n:n + 1], bias=b_scaled[0:S0, n:n + 1])\
                            .then_inc(done, 1)
                passes(b, 0)
                act.wait_ge(scale1_ready, b + 1)
                with act.Fori(0, NK) as j:
                    cols = bass.ds(j * GROUP, GROUP)
                    act.wait_ge(x1_ready, b * NG + j + 2)
                    act.wait_ge(x1_lo_ready, b * NK + j + 1)
                    act.activation(k1a[:, cols], x1[:, cols], ACT.Copy, scale=scale1[:, 0:1])
                    act.activation(x1_full[:, 0, :], x1[:, cols], ACT.Copy, scale=scale1[:, 0:1])
                    act.activation(q1a[0:C, cols], x1[0:C, cols], ACT.Copy, scale=scale1[0:C, 0:1])
                    act.activation(q1b[0:C, cols], x1[0:C, cols], ACT.Copy, scale=scale1[0:C, 0:1])\
                        .then_inc(x1_hi_ready, 1)
                    act.wait_ge(v_psum_ready, (2 * b + 1) * NK + j + 1)
                    act.activation(v32[:, :], proj_ps[:, 0:PER * C], ACT.Copy, scale=factor[:, 3:4])\
                        .then_inc(v32_ready, 1)
                passes(b, 1)

        @block.gpsimd
        def _(pool):
            def split(c, first, count):
                return pool.tensor_tensor(w_rest[:, c, first:first + count], w_exp[:, c, first:first + count],
                                          upper(exp_upper, c, first, count), ALU.subtract)

            def group(b, layer, g):
                n = tile0(b, layer, g)
                with pool.Fori(0, NK) as kt:
                    for c in (0, 2):
                        pool.wait_ge(exp_ready, n + kt * PER + c + 1)
                        split(c, 0, GROUP).then_inc(split_p, 1)
                    if layer == 0:
                        pool.wait_ge(exp_ready, n + kt * PER + 4)
                        split(3, 0, POOL_COLS).then_inc(split_p, 1)
                if layer == 0:
                    pool.wait_ge(exp_ready, n + NC + 1)
                    pool.tensor_tensor(e_bank_rest[:, 0, :], e_bank[:, 0, :], upper(bank_upper, 0, 0, GROUP),
                                       ALU.subtract).then_inc(split_p, 1)

            pool.wait_ge(stats_ready, 8)
            pool.partition_all_reduce(stat_all[:, :], stat[:, :], P, RMAX).then_inc(stats_all_ready, 1)
            with pool.Fori(0, B) as b:
                pool.wait_ge(peak_ready, b + 1)
                pool.sem_inc(peak_seen, 1)
                pool.partition_all_reduce(peak_all[:, :], peak[:, :], P, RMAX).then_inc(peak_all_ready, 1)
                with pool.Fori(0, NK) as j:
                    cols = bass.ds(j * GROUP, GROUP)
                    pool.wait_ge(theta_ready, b * NK + j + 1)
                    pool.tensor_tensor(q0[I:2 * I, cols], full32[I:2 * I, 0, :], q0[I:2 * I, cols],
                                       ALU.subtract)
                    pool.wait_ge(phi_ready, b * NK + j + 1)
                    pool.tensor_tensor(k0[2 * I:S0, cols], full32[2 * I:S0, 1, :], k0[2 * I:S0, cols],
                                       ALU.subtract).then_inc(stack0_ready, 1)
                with pool.Fori(0, NG) as g:
                    group(b, 0, g)
                with pool.Fori(0, NK) as j:
                    cols = bass.ds(j * GROUP, GROUP)
                    pool.wait_ge(x1_hi_ready, b * NK + j + 1)
                    pool.tensor_tensor(k1b[0:C, cols], x1_full[0:C, 0, :], k1a[0:C, cols], ALU.subtract)
                    pool.tensor_tensor(q1a[C:P, cols], x1_full[C:P, 0, :], k1a[C:P, cols], ALU.subtract)\
                        .then_inc(x1_lo_ready, 1)
                with pool.Fori(0, NG) as g:
                    group(b, 1, g)

        @block.vector
        def _(v):
            def powers(peaks, width):
                bits = peaks.bitcast(U32)
                v.tensor_scalar(pow_dn[:, 0:width].bitcast(U32), bits, EXPONENT, None, ALU.bitwise_and)
                return v.tensor_scalar(pow_up[:, 0:width].bitcast(U32), bits, EXPONENT, EXPONENT,
                                       ALU.bitwise_xor, ALU.bitwise_and)

            def image_scales(b):
                n = b * 11
                v.tensor_reduce(peak[:, :], x_sb[:, :], AX_X, ALU.max, apply_absolute_value=True)\
                    .then_inc(peak_ready, 1)
                v.wait_ge(peak_all_ready, b + 1)
                v.scalar_tensor_tensor(bound[:, 0:3], stat_all[:, 0:3], peak_all[:, 0:1], stat_all[:, 6:9],
                                       ALU.mult, ALU.add).then_inc(scale_step, 1)
                v.tensor_copy(bound[:, 3:4], peak_all[:, :]).then_inc(scale_step, 1)
                v.wait_ge(scale_step, n + 2)
                v.scalar_tensor_tensor(bound[:, 4:5], bound[:, 2:3], stat_all[:, 4:5], out_const[:, :],
                                       ALU.mult, ALU.add).then_inc(scale_step, 1)
                v.wait_ge(scale_step, n + 3)
                v.tensor_tensor(bound[:, 4:5], bound[:, 4:5], peak_all[:, :], ALU.add).then_inc(scale_step, 1)
                v.wait_ge(scale_step, n + 4)
                v.tensor_tensor(bound[:, 5:6], bound[:, 4:5], stat_all[:, 3:4], ALU.mult).then_inc(scale_step, 1)
                v.wait_ge(scale_step, n + 5)
                v.tensor_scalar(bound[:, :], bound[:, :], TINY, None, ALU.max).then_inc(scale_step, 1)
                v.wait_ge(scale_step, n + 6)
                powers(bound[:, :], 6).then_inc(scale_step, 1)
                v.wait_ge(scale_step, n + 7)
                v.tensor_scalar(scale0[:, :], pow_up[:, 0:4], 4.0, None, ALU.mult)
                v.tensor_scalar(inv0[:, :], pow_dn[:, 0:4], 0.125, None, ALU.mult)
                v.tensor_scalar(scale1[:, :], pow_up[:, 4:6], 4.0, None, ALU.mult)
                v.tensor_scalar(inv1[:, :], pow_dn[:, 4:6], 0.125, None, ALU.mult).then_inc(scale_step, 1)
                v.wait_ge(scale_step, n + 8)
                v.scalar_tensor_tensor(factor[:, 0:3], scale0[:, 0:3], inv0[:, 3:4], w_i[:, 0:3],
                                       ALU.mult, ALU.mult)
                v.scalar_tensor_tensor(factor[:, 3:4], scale1[:, 1:2], inv1[:, 0:1], w_i[:, 3:4],
                                       ALU.mult, ALU.mult)
                v.tensor_tensor(b_scaled[:, :], b_stat[:, 0:2], scale0[:, 0:2], ALU.mult)
                v.tensor_scalar(g_bias_scaled[:, :], g_bias[:, :], scale0[:, 2:3], None, ALU.mult)
                v.tensor_tensor(logit[:, 0:1], inv0[:, 0:1], inv0[:, 1:2], ALU.mult)
                v.scalar_tensor_tensor(logit[:, 1:2], inv0[:, 1:2], BANK_SCALE, w_i[:, 4:5],
                                       ALU.mult, ALU.mult)
                v.tensor_tensor(logit[:, 2:3], inv1[:, 0:1], inv1[:, 0:1], ALU.mult)
                v.scalar_tensor_tensor(lift[:, 0:1], scale0[:, 0:1], LIFT, scale0[:, 1:2],
                                       ALU.mult, ALU.mult).then_inc(scale_step, 1)
                v.scalar_tensor_tensor(lift[:, 1:2], scale0[:, 1:2], LIFT / BANK_SCALE, w_s[:, 4:5],
                                       ALU.mult, ALU.mult)
                v.scalar_tensor_tensor(lift[:, 2:3], scale1[:, 0:1], LIFT, scale1[:, 0:1],
                                       ALU.mult, ALU.mult).then_inc(scale_step, 1)
                v.wait_ge(scale_step, n + 10)
                v.tensor_scalar(lift[:, :], lift[:, :], LIFT_MOST, None, ALU.min).then_inc(scale_step, 1)
                v.wait_ge(scale_step, n + 11)
                v.memset(recip[:, :], 1.0).then_inc(scale0_ready, 1)

            def values(b, layer, j):
                n = 2 * b * NK + layer * NK + j
                w = (I, C)[layer]
                here = v32[:, 0:PER * w]
                if layer == 0:
                    v.wait_ge(v_psum_ready, n + 1)
                    v.scalar_tensor_tensor(here, proj_ps[:, 0:PER * w], factor[:, 2:3], g_bias_scaled[:, :],
                                           ALU.mult, ALU.add).then_inc(v32_ready, 1)
                v.wait_ge(v32_ready, n + 1)
                here = here.rearrange("p (i c) -> p i c", c=w)
                chunks = bass.ds(j * PER, PER)
                dst = (v0, v1)[layer]
                lo = (I, C + 1)[layer]
                v.tensor_copy(dst[:, chunks, 0:w], here).then_inc(v_hi_ready, 1)
                v.wait_ge(v_hi_ready, n + 1)
                v.tensor_tensor(dst[:, chunks, lo:lo + w], here, dst[:, chunks, 0:w], ALU.subtract)\
                    .then_inc(v_ready, 1)

            def row_max(b, layer, g, kt, i):
                v.wait_ge(row_ready, tile0(b, layer, g) + kt * PER + i + 1)
                v.tensor_reduce(max_part[:, i, bass.ds(kt, 1)], row_ps[:, i % 2, :], AX_X, ALU.max)\
                    .then_inc(row_free, 1)

            def bank_row_max(b, g, t):
                v.wait_ge(row_ready, tile0(b, 0, g) + NC + t + 1)
                v.tensor_reduce(neg_max[:, PER + 2 * t:PER + 2 * t + 2],
                                row_ps[:, t, :].rearrange("p (i k) -> p i k", k=BANK),
                                AX_X, ALU.max, negate=True).then_inc(row_free, 1)

            def group_maxima(b, layer, g):
                n = group_no(b, layer, g)
                v.wait_ge(row_free, tile0(b, layer, g) + T[layer] + 2)
                v.tensor_reduce(neg_max[:, 0:PER], max_part[:, :, :], AX_X, ALU.max, negate=True)\
                    .then_inc(neg_max_ready, 1)
                v.wait_ge(neg_max_ready, n + 1)
                spans = [(0, PER, (0, 2)[layer])] + ([(PER, 2 * PER, 1)] if layer == 0 else [])
                for a, e, s in spans:
                    op = v.tensor_scalar(max_cols[:, a:e, 0], neg_max[:, a:e], lift[:, s:s + 1], None, ALU.add)
                op.then_inc(max_hi_ready, 1)
                v.wait_ge(max_hi_ready, n + 1)
                for a, e, s in spans:
                    op = v.scalar_tensor_tensor(max_cols[:, a:e, 1], neg_max[:, a:e], lift[:, s:s + 1],
                                                max_cols[:, a:e, 0], ALU.add, ALU.subtract)
                op.then_inc(max_cols_ready, 1)

            def split(c, first, count):
                return v.tensor_tensor(w_rest[:, c, first:first + count], w_exp[:, c, first:first + count],
                                       upper(exp_upper, c, first, count), ALU.subtract)

            def split_after(b, layer, g, kt, c):
                if c % 2:
                    return
                v.wait_ge(exp_ready, tile0(b, layer, g) + kt * PER + c + 2)
                if layer == 0 and c == 2:
                    split(3, POOL_COLS, GROUP - POOL_COLS).then_inc(split_v, 1)
                else:
                    split(c + 1, 0, GROUP).then_inc(split_v, 1)

            def steps(b, layer, g, kt, nxt, after=()):
                for c in range(PER):
                    if nxt:
                        row_max(b, layer, g + 1, kt + 1, c)
                    split_after(b, layer, g, kt, c)
                    for at, do in after:
                        if at == c:
                            do()

            def last_steps(b, layer, g, nxt, nxt2):
                kt = NK - 1
                rows_from = T[layer] - PER
                for s in range(kt * PER, T[layer]):
                    if s < rows_from and nxt:
                        bank_row_max(b, g + 1, s - kt * PER)
                    if s == rows_from and nxt:
                        group_maxima(b, layer, g + 1)
                    if s >= rows_from and nxt2:
                        row_max(b, layer, g + 2, 0, s - rows_from)
                    if s < NC:
                        split_after(b, layer, g, kt, s - kt * PER)
                    elif s == NC:
                        v.wait_ge(exp_ready, tile0(b, 0, g) + NC + 2)
                        v.tensor_tensor(e_bank_rest[:, 1, :], e_bank[:, 1, :], upper(bank_upper, 1, 0, GROUP),
                                        ALU.subtract).then_inc(split_v, 1)

            def normalise(b, layer, g):
                n = group_no(b, layer, g)
                done = b * NG * 3 + layer * NG * 2 + g * (2, 1)[layer]
                w = MAIN[layer]
                main = acc_sb[:, 0:PER * w].rearrange("p (q w) -> p q w", w=w)
                v.wait_ge(acc_free, n + 2)
                by = recip[:, 0:PER].unsqueeze(2)
                if layer:
                    v.reciprocal(recip[:, 0:PER], main[:, :, C]).then_inc(norm_step, 1)
                    v.wait_ge(norm_step, done + 1)
                    v.scalar_tensor_tensor(y_norm[:, :, :], main[:, :, 0:C], inv1[:, 1:2],
                                           by.broadcast_to([P, PER, C]), ALU.mult, ALU.mult)\
                        .then_inc(y_ready, 1)
                    return
                side = acc_sb[:, PER * w:].rearrange("p (q w) -> p q w", w=BANKW)
                half = y_sum[:, :].rearrange("p (q c) -> p q c", c=I)
                v.reciprocal(recip[:, 0:PER], main[:, :, 2 * I])
                v.reciprocal(recip[:, PER:], side[:, :, I]).then_inc(norm_step, 1)
                v.tensor_tensor(half, main[:, :, 0:I], main[:, :, I:2 * I], ALU.add).then_inc(norm_step, 1)
                v.wait_ge(norm_step, done + 2)
                v.scalar_tensor_tensor(y_norm[:, :, 0:I], half, inv0[:, 2:3],
                                       by.broadcast_to([P, PER, I]), ALU.mult, ALU.mult)
                v.scalar_tensor_tensor(y_norm[:, :, I:C], side[:, :, 0:I], w_i[:, 4:5],
                                       recip[:, PER:].unsqueeze(2).broadcast_to([P, PER, I]),
                                       ALU.mult, ALU.mult).then_inc(y_ready, 1)

            def take_rows(b, layer, g):
                v.wait_ge(yt_psum_ready, group_no(b, layer, g) + 1)
                cols = bass.ds(g * GROUP, GROUP)
                if layer == 0:
                    v.tensor_copy(y_t[:, :], turn_ps[0:C, :]).then_inc(yt_free, 1)
                else:
                    v.tensor_tensor(out_sb[:, cols], turn_ps[0:C, :], x1[0:C, cols], ALU.add)\
                        .then_inc(yt_free, 1)

            def add_image(b, g):
                cols = bass.ds(g * GROUP, GROUP)
                v.wait_ge(proj_psum_ready, b * NG + g + 1)
                v.scalar_tensor_tensor(x1[:, cols], proj_ps[:, :], b_out[:, :], x_sb[:, cols],
                                       ALU.add, ALU.add).then_inc(x1_ready, 1)

            def head(b, layer, g, nxt, finish):
                steps(b, layer, g, 0, nxt)
                if finish:
                    normalise(b, layer, g - 1)
                steps(b, layer, g, 1, nxt)
                steps(b, layer, g, 2, nxt,
                      [(0, lambda: take_rows(b, layer, g - 1))] if finish else ())
                steps(b, layer, g, 3, nxt,
                      [(1, lambda: add_image(b, g - 1))] if finish and layer == 0 else ())

            def rest(b, layer, g, nxt, nxt2):
                with v.Fori(4, NK - 1) as kt:
                    steps(b, layer, g, kt, nxt)
                last_steps(b, layer, g, nxt, nxt2)

            def passes(b, layer):
                head(b, layer, 0, True, False)
                with v.Fori(0, NG - 2) as g:
                    rest(b, layer, g, True, True)
                    head(b, layer, g + 1, True, True)
                rest(b, layer, NG - 2, True, False)
                head(b, layer, NG - 1, False, True)
                rest(b, layer, NG - 1, False, False)
                normalise(b, layer, NG - 1)
                take_rows(b, layer, NG - 1)
                if layer == 0:
                    add_image(b, NG - 1)

            def row_maxima(b, layer, g, kt):
                for i in range(PER):
                    row_max(b, layer, g, kt, i)

            def fill0(b):
                def tile(j, rows):
                    cols = bass.ds(j * GROUP, GROUP)
                    v.wait_ge(x_hi_ready, b * NK + j + 1)
                    v.scalar_tensor_tensor(x16[C:P, cols], x_sb[C:P, cols], scale0[C:P, 3:4], x16[C:P, cols],
                                           ALU.mult, ALU.subtract).then_inc(x16_ready, 1)
                    if rows:
                        row_maxima(b, 0, 0, j - 1)
                    values(b, 0, j)

                tile(0, False)
                with v.Fori(1, NK) as j:
                    tile(j, True)
                row_maxima(b, 0, 0, NK - 1)
                for t in range(BC):
                    bank_row_max(b, 0, t)
                group_maxima(b, 0, 0)
                row_maxima(b, 0, 1, 0)

            def fill1(b):
                v.wait_ge(out_stored, b * NG * 16)
                v.memset(q1b[C:R1, :], 0.0).then_inc(scale1_ready, 1)
                values(b, 1, 0)
                with v.Fori(1, NK) as j:
                    row_maxima(b, 1, 0, j - 1)
                    values(b, 1, j)
                row_maxima(b, 1, 0, NK - 1)
                group_maxima(b, 1, 0)
                row_maxima(b, 1, 1, 0)

            v.memset(ones2[C:C + 2, :], 1.0).then_inc(consts_set, 1)
            v.memset(zero16[:, :], 0.0).then_inc(consts_set, 1)
            v.memset(k0[S0:R0, :], 1.0).then_inc(consts_set, 1)
            v.memset(k1b[C:R1, :], 1.0).then_inc(consts_set, 1)
            v.memset(v0[:, :, 2 * I:2 * I + 1], 1.0).then_inc(consts_set, 1)
            v.memset(v1[:, :, C:C + 1], 1.0).then_inc(consts_set, 1)
            v.memset(bank_val[:, :, I:I + 1], 1.0).then_inc(consts_set, 1)
            for free, count in ((row_free, 2), (exp_free, PER), (acc_free, 1), (y_ready, 1), (yt_free, 1),
                                (x1_ready, 1), (v_ready, 1), (stack0_ready, 1), (x1_lo_ready, 1)):
                v.sem_inc(free, count)
            v.wait_ge(weights_loaded, WEIGHTS_IN)
            v.tensor_copy(ident16[:, :], ident[:, :]).then_inc(consts_set, 1)
            v.tensor_tensor(b_out[:, :], b_out2[:, 0:1], b_out2[:, 1:2], ALU.add).then_inc(consts_set, 1)
            v.tensor_reduce(stat[:, 0:6], w_stat[:, :, :], AX_X, ALU.add, apply_absolute_value=True)\
                .then_inc(stats_ready, 1)
            v.tensor_reduce(stat[:, 6:11], b_stat[:, :].unsqueeze(2), AX_X, ALU.max,
                            apply_absolute_value=True).then_inc(stats_ready, 1)
            v.tensor_reduce(stat[:, 11:15], w_stat[:, 0:4, :], AX_X, ALU.max, apply_absolute_value=True)\
                .then_inc(stats_ready, 1)
            v.tensor_reduce(stat[:, 15:16], bank[:, :], AX_X, ALU.max, apply_absolute_value=True)\
                .then_inc(stats_ready, 5)
            v.wait_ge(stats_all_ready, 1)
            v.tensor_tensor(out_const[:, :], stat_all[:, 15:16], stat_all[:, 5:6], ALU.mult)\
                .then_inc(setup_step, 1)
            v.wait_ge(setup_step, 1)
            for n in (9, 10):
                v.tensor_tensor(out_const[:, :], out_const[:, :], stat_all[:, n:n + 1], ALU.add)\
                    .then_inc(setup_step, 1)
                v.wait_ge(setup_step, n - 7)
            v.tensor_scalar(w_clamp[:, :], stat_all[:, 11:16], TINY, None, ALU.max).then_inc(setup_step, 1)
            v.wait_ge(setup_step, 4)
            powers(w_clamp[:, :], 5).then_inc(setup_step, 1)
            v.wait_ge(setup_step, 5)
            v.tensor_scalar(w_s[:, :], pow_up[:, 0:5], 4.0, None, ALU.mult)
            v.tensor_scalar(w_i[:, :], pow_dn[:, 0:5], 0.125, None, ALU.mult).then_inc(setup_step, 1)
            v.wait_ge(setup_step, 6)
            for n, (c0, c1) in enumerate(WCOLS):
                v.tensor_scalar(w_scaled[:, c0:c1], w_proj[:, c0:c1], w_s[:, n:n + 1], None, ALU.mult)
            v.tensor_scalar(bank_t[:, :, :], bank_t[:, :, :], w_s[:, 4:5], None, ALU.mult)
            v.tensor_scalar(bank32[:, :], bank[:, :], w_s[:, 4:5], None, ALU.mult).then_inc(setup_step, 1)
            v.wait_ge(setup_step, 7)
            v.tensor_copy(w16[:, 0, :], w_scaled[:, :])
            v.tensor_copy(bank_val[:, :, 0:I], bank_t[:, :, :])
            v.tensor_copy(bank_stack[:, :], bank32[:, :]).then_inc(setup_step, 1)
            v.wait_ge(setup_step, 8)
            v.tensor_tensor(w16[:, 1, :], w_scaled[:, :], w16[:, 0, :], ALU.subtract)
            v.tensor_tensor(bank_val[:, :, I + 1:], bank_t[:, :, :], bank_val[:, :, 0:I],
                            ALU.subtract).then_inc(consts_set, 3)
            v.tensor_tensor(bank_stack[I:2 * I, :], bank32[I:2 * I, :], bank_stack[I:2 * I, :],
                            ALU.subtract).then_inc(setup_step, 1)
            with v.Fori(0, B) as b:
                v.wait_ge(x_loaded, (b + 1) * 32)
                image_scales(b)
                fill0(b)
                passes(b, 0)
                fill1(b)
                passes(b, 1)


def kernel(x, L0_conv_g_w, L0_conv_g_b, L0_conv_theta_w, L0_conv_theta_b, L0_conv_phi_w, L0_conv_phi_b,
           L0_conv_W_w, L0_conv_W_b, L0_conv_Wz1_w, L0_conv_Wz1_b, L0_conv_mb, L1_conv_weight):
    import numpy as np
    import concourse.bacc as bacc
    from concourse.bass_utils import run_bass_kernel_spmd

    def a(t):
        return np.asarray(t)

    def rows(t):
        full = np.zeros((P, c), np.float32)
        full[:, :t.shape[1]] = np.tile(t, (P // t.shape[0], 1))
        return full

    nb, c, h, w = x.shape
    inter = L0_conv_g_w.shape[0]
    chunks = L0_conv_mb.shape[1] // P
    theta_t, phi_t = a(L0_conv_theta_w).T, a(L0_conv_phi_w).T
    weights = np.concatenate([theta_t] * 3 + [phi_t] * 3 + [a(L0_conv_g_w).T, a(L1_conv_weight)], axis=1)
    arrays = {
        "x": a(x).reshape(nb, c, h * w),
        "weights": np.tile(weights, (2, 1)),
        "wstat": np.stack([rows(a(t)) for t in (L0_conv_theta_w, L0_conv_phi_w, L0_conv_g_w,
                                                a(L1_conv_weight).T, L0_conv_W_w, L0_conv_Wz1_w)], axis=1),
        "bstat": np.stack([np.tile(a(t), P // t.shape[0]) for t in (
            L0_conv_theta_b, L0_conv_phi_b, L0_conv_g_b, L0_conv_W_b, L0_conv_Wz1_b)], axis=1),
        "out_w": np.concatenate([np.tile(a(L0_conv_W_w).T, (1, 2)), np.tile(a(L0_conv_Wz1_w).T, (1, 2))], axis=0),
        "out_b": np.stack([np.tile(a(L0_conv_W_b), 2), np.tile(a(L0_conv_Wz1_b), 2)], axis=1),
        "g_bias": np.tile(a(L0_conv_g_b), (P, GROUP // P)),
        "bank": np.tile(a(L0_conv_mb), (P // inter, 1)),
        "bank_t": a(L0_conv_mb).T.reshape(chunks, P, inter).transpose(1, 0, 2),
        "ident": np.eye(P, dtype=np.float32),
    }
    arrays = {name: np.ascontiguousarray(t) for name, t in arrays.items()}
    nc = bacc.Bacc("TRN2", target_bir_lowering=False, num_devices=1)
    args = [nc.dram_tensor(f"{name}_dram", t.shape, mybir.dt.from_np(t.dtype), kind="ExternalInput").ap()
            for name, t in arrays.items()]
    out = nc.dram_tensor("out_dram", arrays["x"].shape, F32, kind="ExternalOutput").ap()
    non_local_then_graph(nc, *args, out)
    r = run_bass_kernel_spmd(nc, [{f"{name}_dram": t for name, t in arrays.items()}], core_ids=[0])
    return r.results[0]["out_dram"].reshape(nb, c, h, w)
```

```python
from contextlib import ExitStack

import concourse.bass as bass
from concourse import mybir

ALU = mybir.AluOpType
ACT = mybir.ActivationFunctionType
AX_X = mybir.AxisListType.X
F32 = mybir.dt.float32
F16 = mybir.dt.float16
BF16 = mybir.dt.bfloat16
U32 = mybir.dt.uint32
RMAX = bass.bass_isa.ReduceOp.max

P = 128
GROUP = 512
EXPONENT = 0x7F800000
TINY = 1e-30
LIFT = 8 * 0.6931471805599453
LIFT_MOST = 16000.0


def non_local_then_graph(nc, x, weights_in, wstat_in, bstat_in, out_w_in, out_b_in, g_bias_in,
                         bank_in, bank_t_in, ident_in, out):
    B, C, N = x.shape
    I = C // 2
    NG = N // GROUP
    NK = N // GROUP
    NC = N // P
    PER = GROUP // P
    BANK = bank_in.shape[1]
    BC = BANK // P
    S0 = 3 * I
    R0 = S0 + 2
    R1 = C + 2
    MAIN = [2 * I + 1, C + 1]
    BANKW = I + 1
    WIDE = PER - 1
    ACC = [PER * (MAIN[0] + BANKW), WIDE * (2 * C + 1) + MAIN[1]]
    T = [NC + BC, NC]
    BANK_SCALE = float(I) ** -0.5
    WCOLS = [(0, S0), (S0, 2 * S0), (2 * S0, 2 * S0 + I), (2 * S0 + I, 2 * S0 + I + C)]
    HEAD = 5
    assert S0 <= 96 and BC == 2 and PER == 4 and NG == NK and B > 2

    POOL_CHUNKS, EASY = [(0, 2, 3), (0, 2), (0, 2)], 2

    def splits_of(who, share):
        chunks = len(POOL_CHUNKS[share]) if who else PER - len(POOL_CHUNKS[share])
        return NK * chunks + (share != 1)

    def group_no(b, g):
        return b * NG + g

    def tile0(b, layer, g):
        return group_no(b, g) * T[layer]

    def alone(b):
        return isinstance(b, int)

    def share_of(b, layer, g):
        return EASY if layer == 0 and (alone(b) or isinstance(g, int) and g == NG - 1) else layer

    def splits0(who, b, layer, g):
        if layer == 1:
            return group_no(b, g) * splits_of(who, 1)
        if alone(b):
            return g * splits_of(who, EASY)
        per_image = (NG - 1) * splits_of(who, 0) + splits_of(who, EASY)
        return (NG * splits_of(who, EASY) - per_image) + b * per_image + g * splits_of(who, 0)

    def last_order(live):
        if len(live) == 1:
            (layer, b), = live
            return [(layer, b, s) for s in range(NC - PER, T[layer])]
        (_, b1), (_, b0) = live
        return [(layer, (b0, b1)[layer], NC - PER + s) for layer, s in (
            (1, 0), (0, 0), (1, 1), (0, 1), (0, 2), (1, 2), (0, 3), (1, 3), (0, 4), (0, 5))]

    with ExitStack() as ctx:
        def sb(name, shape, dt):
            return ctx.enter_context(nc.sbuf_tensor(name, shape, dt))

        def psum(name, shape, dt):
            return ctx.enter_context(nc.psum_tensor(name, shape, dt))

        def sem(name):
            return ctx.enter_context(nc.semaphore(name))

        def sem_pair(name):
            return [sem(f"{name}_{layer}") for layer in range(2)]

        WALL = WCOLS[-1][1]
        w_proj = sb("w_proj", [P, WALL], F32)
        w_scaled = sb("w_scaled", [P, WALL], F32)
        w16 = sb("w16", [P, 2, WALL], F16)
        w_stat = sb("w_stat", [P, 6, C], F32)
        b_stat = sb("b_stat", [P, 5], F32)
        w_out = sb("w_out", [C, 2 * C], F32)
        b_out2 = sb("b_out2", [P, 2], F32)
        b_out = sb("b_out", [P, 1], F32)
        g_bias = sb("g_bias", [P, PER * I], F32)
        bank = sb("bank", [P, BANK], F32)
        bank_t = sb("bank_t", [P, BC, I], F32)
        bank_val = sb("bank_val", [P, BC, 2 * I + 1], F16)
        ident = sb("ident", [P, P], F32)
        ident16 = sb("ident16", [P, P], F16)
        ones2 = sb("ones2", [C + 2, P], F16)
        zero16 = sb("zero16", [32, GROUP], F16)
        x_sb = sb("x_sb", [P, N], F32)
        x16 = sb("x16", [P, N], F16)
        full32 = sb("full32", [S0, 2, GROUP], F32)
        q0 = sb("q0", [P, N], F16)
        k0 = sb("k0", [P, N], F16)
        bank32 = sb("bank32", [P, BANK], F32)
        bank_stack = sb("bank_stack", [P, BANK], F16)
        x_keep = sb("x_keep", [P, GROUP], F32)
        v0 = sb("v0", [P, NC, 2 * I + 1], F16)
        v32 = [sb("v32_0", [P, PER * I], F32), sb("v32_1", [P, PER * C], F32)]
        x1 = sb("x1", [P, N], F32)
        x1_full = sb("x1_full", [P, GROUP], F32)
        q1a = sb("q1a", [P, N], F16)
        k1a = sb("k1a", [P, N], F16)
        q1b = sb("q1b", [P, N], F16)
        k1b = sb("k1b", [P, N], F16)
        v1 = sb("v1", [P, NC, 2 * C + 1], F16)
        out_sb = sb("out_sb", [C, N], F32)
        w_exp = [sb(f"w_exp_{n}", [P, PER, GROUP], F32) for n in range(2)]
        w_rest = [sb(f"w_rest_{n}", [P, PER, GROUP], F16) for n in range(2)]
        e_bank = sb("e_bank", [P, BC, GROUP], F32)
        e_bank_rest = sb("e_bank_rest", [P, BC, GROUP], F16)
        bank_max = sb("bank_max", [C + 2, GROUP], F16)
        max_part = [sb(f"max_part_{n}", [P, PER, NK], F32) for n in range(2)]
        neg_max = [sb(f"neg_max_{n}", [P, 2 * PER], F32) for n in range(2)]
        max_cols = [sb(f"max_cols_{n}", [P, 2 * PER, 2], F16) for n in range(2)]
        acc_sb = [sb(f"acc_sb_{n}", [P, ACC[n]], F32) for n in range(2)]
        recip = [sb(f"recip_{n}", [P, 2 * PER], F32) for n in range(2)]
        y_sum = sb("y_sum", [P, PER * I], F32)
        y_sum1 = sb("y_sum1", [P, WIDE * C], F32)
        y_norm = [sb(f"y_norm_{n}", [P, PER, C], F32) for n in range(2)]
        y_t = sb("y_t", [C, GROUP], F32)
        NSTAT = 6 + 5 + 4 + 1
        stat = sb("stat", [P, NSTAT], F32)
        stat_all = sb("stat_all", [P, NSTAT], F32)
        peak_part = sb("peak_part", [P, NG], F32)
        peak = sb("peak", [P, 1], F32)
        peak_all = sb("peak_all", [P, 1], F32)
        out_const = sb("out_const", [P, 1], F32)
        bound = sb("bound", [P, 6], F32)
        w_clamp = sb("w_clamp", [P, 5], F32)
        pow_up = sb("pow_up", [P, 6], F32)
        pow_dn = sb("pow_dn", [P, 6], F32)
        w_s = sb("w_s", [P, 5], F32)
        w_i = sb("w_i", [P, 5], F32)
        SCALES = 24
        scales_next = sb("scales_next", [P, SCALES], F32)
        scales_now = sb("scales_now", [P, SCALES], F32)
        scales1 = sb("scales1", [P, 7], F32)
        g_bias_scaled = sb("g_bias_scaled", [P, PER * I], F32)

        def layer0_scales(tile):
            return [tile[:, a:e] for a, e in ((0, 4), (4, 8), (8, 11), (11, 13), (13, 15), (15, 17))]

        scale0, inv0, factor, b_scaled, logit, lift = layer0_scales(scales_now)
        SC1, INV1, FACTOR1, LOGIT1, LIFT1 = (slice(0, 2), slice(2, 4), slice(4, 5), slice(5, 6), slice(6, 7))

        row_ps = psum("row_ps", [P, 2, GROUP], F32)
        col_ps = psum("col_ps", [P, 2, GROUP], F32)
        acc_ps = [psum(f"acc_ps_{n}", [P, GROUP], F32) for n in range(2)]
        turn_ps = psum("turn_ps", [P, GROUP], F32)
        proj_ps = psum("proj_ps", [P, GROUP], F32)
        theta_ps, v0_ps = col_ps[:, 0, :], col_ps[:, 1, :]
        phi_ps, v1_ps = acc_ps

        weights_loaded = sem("weights_loaded")
        x_loaded = sem("x_loaded")
        x_last_loaded = sem("x_last_loaded")
        out_stored = sem("out_stored")
        consts_set = sem("consts_set")
        stats_ready = sem("stats_ready")
        stats_all_ready = sem("stats_all_ready")
        setup_step = sem("setup_step")
        peak_part_ready = sem("peak_part_ready")
        image_kept = sem("image_kept")
        peak_ready = sem("peak_ready")
        peak_seen = sem("peak_seen")
        peak_all_ready = sem("peak_all_ready")
        scale_step = sem("scale_step")
        scale0_ready = sem("scale0_ready")
        scale1_ready = sem("scale1_ready")
        clear_seen = sem("clear_seen")
        q1b_cleared = sem("q1b_cleared")
        x_hi_ready = sem("x_hi_ready")
        x16_ready = sem("x16_ready")
        theta_psum_ready = sem("theta_psum_ready")
        phi_psum_ready = sem("phi_psum_ready")
        v_psum_ready = sem_pair("v_psum_ready")
        theta_ready = sem("theta_ready")
        phi_ready = sem("phi_ready")
        v32_ready = sem_pair("v32_ready")
        v_hi_ready = sem_pair("v_hi_ready")
        v_ready = sem_pair("v_ready")
        stack0_ready = sem("stack0_ready")
        x1_hi_ready = sem("x1_hi_ready")
        x1_lo_ready = sem("x1_lo_ready")
        row_ready = sem_pair("row_ready")
        row_free = sem_pair("row_free")
        col_ready = sem_pair("col_ready")
        exp_ready = sem_pair("exp_ready")
        exp_free = sem_pair("exp_free")
        split_v = sem_pair("split_v")
        split_p = sem_pair("split_p")
        neg_max_ready = sem_pair("neg_max_ready")
        max_hi_ready = sem_pair("max_hi_ready")
        max_cols_ready = sem_pair("max_cols_ready")
        max_psum_ready = sem_pair("max_psum_ready")
        max_rows_ready = sem_pair("max_rows_ready")
        bank_max_ready = sem("bank_max_ready")
        acc_free = sem_pair("acc_free")
        norm_step = sem_pair("norm_step")
        y_ready = sem_pair("y_ready")
        y_seen = sem("y_seen")
        yt_psum_ready = sem_pair("yt_psum_ready")
        yt_free = sem_pair("yt_free")
        proj_psum_ready = sem("proj_psum_ready")
        x1_ready = sem("x1_ready")

        WEIGHT_LOADS = [
            (w_proj[:, :], weights_in[:, :]), (w_stat[:, :, :], wstat_in[:, :, :]),
            (b_stat[:, :], bstat_in[:, :]), (w_out[:, :], out_w_in[:, :]),
            (b_out2[:, :], out_b_in[:, :]), (g_bias[:, :], g_bias_in[:, :]),
            (bank[:, :], bank_in[:, :]), (bank_t[:, :, :], bank_t_in[:, :, :]),
            (ident[:, :], ident_in[:, :]),
        ]
        WEIGHTS_IN = len(WEIGHT_LOADS) * 16
        CONSTS, SETUP = 12, 9

        exp_upper = [w_exp[n][:, :, :].bitcast(BF16) for n in range(2)]
        bank_upper = e_bank[:, :, :].bitcast(BF16)

        def upper(view, slot, first, count):
            return view[:, slot, 2 * first + 1:2 * (first + count):2]

        def row_bank_of(b, layer, i, spare):
            if spare and i % 2:
                return (proj_ps, turn_ps)[layer][:, :]
            return row_ps[:, i % 2 if alone(b) and not spare else layer, :]

        def col_bank_of(b, layer, c):
            return col_ps[:, c % 2 if alone(b) else layer, :]

        block = ctx.enter_context(nc.Block())

        @block.sync
        def _(sp):
            def load_group(b, g, done):
                cols = bass.ds(g * GROUP, GROUP)
                for half in range(2):
                    sp.dma_start(x_sb[half * C:(half + 1) * C, cols],
                                 x[bass.ds(b, 1), :, cols].rearrange("a c n -> (a c) n")).then_inc(done, 16)

            def store_group(b, g):
                cols = bass.ds(g * GROUP, GROUP)
                sp.wait_ge(yt_free[1], group_no(b, g) + 2)
                sp.dma_start(out[bass.ds(b, 1), :, cols].rearrange("a c n -> (a c) n"),
                             out_sb[:, cols]).then_inc(out_stored, 16)

            sp.sem_inc(out_stored, 16)
            with sp.Fori(0, NG - 1) as g:
                load_group(0, g, x_loaded)
            load_group(0, NG - 1, x_last_loaded)
            for dst, src in WEIGHT_LOADS:
                sp.dma_start(dst, src).then_inc(weights_loaded, 16)
            with sp.Fori(0, NG - 1) as g:
                sp.wait_ge(x1_ready, group_no(0, g) + 2)
                load_group(1, g, x_loaded)
            sp.wait_ge(image_kept, 1)
            load_group(1, NG - 1, x_last_loaded)
            with sp.Fori(0, B - 2) as b:
                with sp.Fori(0, NG - 1) as g:
                    store_group(b, g)
                    sp.wait_ge(x1_ready, group_no(b + 1, g) + 2)
                    load_group(b + 2, g, x_loaded)
                sp.wait_ge(image_kept, b + 2)
                load_group(b + 2, NG - 1, x_last_loaded)
                store_group(b, NG - 1)
            sp.sem_inc(x_loaded, (NG - 1) * 32)
            sp.sem_inc(x_last_loaded, 32)
            with sp.Fori(B - 2, B) as b:
                with sp.Fori(0, NG) as g:
                    store_group(b, g)
            sp.wait_ge(out_stored, (B * NG + 1) * 16)

        @block.tensor
        def _(pe):
            def row_tile(b, layer, g, kt, i, spare=False):
                two_banks = spare or alone(b)
                pe.wait_ge(row_free[layer], tile0(b, layer, g) + kt * PER + i + (1 if two_banks else 2))
                ps = row_bank_of(b, layer, i, spare)
                queries = bass.ds(g * GROUP + i * P, P)
                keys = bass.ds(kt * GROUP, GROUP)
                if layer == 0:
                    mm = pe.matmul(ps, q0[0:S0, queries], k0[0:S0, keys],
                                   start=True, stop=True)
                else:
                    pe.matmul(ps, q1a[:, queries], k1a[:, keys], start=True, stop=False)
                    mm = pe.matmul(ps, q1b[0:R1, queries], k1b[0:R1, keys],
                                   start=False, stop=True)
                mm.then_inc(row_ready[layer], 1)

            def row_bank(b, g, t):
                pe.wait_ge(row_free[0], tile0(b, 0, g) + NC + t + (1 if alone(b) else 2))
                ps = row_bank_of(b, 0, t, False)
                for i in range(2):
                    mm = pe.matmul(ps[:, i * BANK:(i + 1) * BANK],
                                   k0[0:S0, bass.ds(g * GROUP + (2 * t + i) * P, P)],
                                   bank_stack[0:S0, :], start=True, stop=True)
                mm.then_inc(row_ready[0], 1)

            def col_tile(b, layer, g, kt, c):
                keys = bass.ds(kt * GROUP + c * P, P)
                queries = bass.ds(g * GROUP, GROUP)
                ps = col_bank_of(b, layer, c)
                if layer == 0:
                    mm = pe.matmul(ps, k0[0:R0, keys], q0[0:R0, queries],
                                   start=True, stop=True)
                else:
                    pe.matmul(ps, k1a[:, keys], q1a[:, queries], start=True, stop=False)
                    mm = pe.matmul(ps, k1b[0:R1, keys], q1b[0:R1, queries],
                                   start=False, stop=True)
                mm.then_inc(col_ready[layer], 1)

            def col_bank(b, g, c):
                if c == 0:
                    pe.wait_ge(bank_max_ready, group_no(b, g) + 1)
                ps = col_bank_of(b, 0, c)
                pe.matmul(ps, bank_stack[0:S0, c * P:(c + 1) * P],
                          k0[0:S0, bass.ds(g * GROUP, GROUP)], start=True, stop=False)
                pe.matmul(ps, ones2[C:C + 2, :], bank_max[C:C + 2, :],
                          start=False, stop=True).then_inc(col_ready[0], 1)

            def weigh(b, layer, g, kt, c, last):
                by_pool = POOL_CHUNKS[share_of(b, layer, g)]
                if c in by_pool:
                    pe.wait_ge(split_p[layer], splits0(1, b, layer, g) + len(by_pool) * kt + by_pool.index(c) + 1)
                else:
                    by_v = [n for n in range(PER) if n not in by_pool]
                    pe.wait_ge(split_v[layer], splits0(0, b, layer, g) + len(by_v) * kt + by_v.index(c) + 1)
                chunk = bass.ds(kt * PER + c, 1)
                values = (v0, v1)[layer][:, chunk, :].rearrange("p a w -> p (a w)")
                w = (MAIN[0], 2 * C + 1)[layer]
                for i in range(PER):
                    for part in (upper(exp_upper[layer], c, i * P, P), w_rest[layer][:, c, i * P:(i + 1) * P]):
                        if layer == 0 or i < WIDE:
                            at = acc_ps[layer][:, i * w:(i + 1) * w]
                            mm = pe.matmul(at, part, values, start=False, stop=last, skip_group_check=True)
                        else:
                            at = acc_ps[1][:, i * w:i * w + C + 1]
                            pe.matmul(at, part, values[:, 0:C + 1], start=False, stop=last, skip_group_check=True)
                            mm = pe.matmul(at[:, 0:C], part, values[:, C + 1:],
                                           start=False, stop=last, skip_group_check=True)
                mm.then_inc(exp_free[layer], 1)

            def weigh_bank(b, g, c):
                share = share_of(b, 0, g)
                if c == 0:
                    pe.wait_ge(split_p[0], splits0(1, b, 0, g) + splits_of(1, share))
                else:
                    pe.wait_ge(split_v[0], splits0(0, b, 0, g) + splits_of(0, share))
                for i in range(PER):
                    at = PER * MAIN[0] + i * BANKW
                    for part in (upper(bank_upper, c, i * P, P), e_bank_rest[:, c, i * P:(i + 1) * P]):
                        pe.matmul(acc_ps[0][:, at:at + BANKW], part, bank_val[:, c, 0:BANKW],
                                  start=False, stop=c == BC - 1, skip_group_check=True)
                        mm = pe.matmul(acc_ps[0][:, at:at + I], part, bank_val[:, c, BANKW:],
                                       start=False, stop=c == BC - 1, skip_group_check=True)
                mm.then_inc(exp_free[0], 1)

            def turn_maxima(live, layer, g):
                images = dict(live)
                if layer == 0 and len(live) == 2:
                    pe.wait_ge(max_rows_ready[1], group_no(images[1], g) + 1)
                elif len(live) == 2:
                    pe.wait_ge(bank_max_ready, group_no(images[0], g))
                pe.wait_ge(max_cols_ready[layer], group_no(images[layer], g) + 1)
                row = (S0, C)[layer]
                for i in range(PER):
                    mm = pe.matmul(turn_ps[row:row + 2, i * P:(i + 1) * P], max_cols[layer][:, i, :],
                                   ident16[:, :], start=True, stop=True, skip_group_check=True)
                if layer == 0:
                    for i in range(PER):
                        mm = pe.matmul(turn_ps[C:C + 2, i * P:(i + 1) * P], max_cols[0][:, PER + i, :],
                                       ident16[:, :], start=True, stop=True, skip_group_check=True)
                mm.then_inc(max_psum_ready[layer], 1)

            def clear_sums(b, layer, g):
                pe.wait_ge(acc_free[layer], group_no(b, g) + 1)
                pe.matmul(acc_ps[layer][:, 0:ACC[layer]], zero16[:, 0:P], zero16[:, 0:ACC[layer]],
                          start=True, stop=False, skip_group_check=True)

            def steps(live, g, kt, nxt, after=None):
                for c in range(PER):
                    for layer, b in live:
                        if nxt:
                            row_tile(b, layer, g + 1, kt + 1, c)
                        pe.wait_ge(exp_ready[layer], tile0(b, layer, g) + kt * PER + c + (1 if alone(b) else 2))
                        col_tile(b, layer, g, kt, c + 2)
                        if after and c == 0 and after.get("clear"):
                            clear_sums(b, layer, g)
                        weigh(b, layer, g, kt, c, False)
                    if after and c in after:
                        after[c]()

            def last_steps(live, g, nxt, nxt2):
                kt = NK - 1
                for layer, b, s in last_order(live):
                    rows_from = T[layer] - PER
                    if s < rows_from and nxt:
                        row_bank(b, g + 1, s - kt * PER)
                    if s >= rows_from and nxt2:
                        row_tile(b, layer, g + 2, 0, s - rows_from)
                    ahead = s + 2
                    if ahead < T[layer] or nxt:
                        pe.wait_ge(exp_ready[layer], tile0(b, layer, g) + s + (1 if alone(b) else 2))
                    if ahead < NC:
                        col_tile(b, layer, g, kt, ahead - kt * PER)
                    elif ahead < T[layer]:
                        col_bank(b, g, ahead - NC)
                    elif nxt:
                        if ahead == T[layer]:
                            pe.wait_ge(max_rows_ready[layer], group_no(b, g + 1) + 1)
                        col_tile(b, layer, g + 1, 0, ahead - T[layer])
                    if s < NC:
                        weigh(b, layer, g, kt, s - kt * PER, s == NC - 1)
                    else:
                        weigh_bank(b, g, s - NC)
                    if nxt and s == rows_from:
                        turn_maxima(live, layer, g + 1)

            def turn_rows(live, layer, g):
                images = dict(live)
                n = group_no(images[layer], g)
                if len(live) == 1:
                    pe.wait_ge(yt_free[layer], n + 1)
                elif layer == 0:
                    pe.wait_ge(yt_free[1], group_no(images[1], g) + 2)
                else:
                    pe.wait_ge(yt_free[0], group_no(images[0], g) + 1)
                pe.wait_ge(y_ready[layer], n + 2)
                pe.sem_inc(y_seen, 1)
                for i in range(PER):
                    mm = pe.transpose(turn_ps[0:C, i * P:(i + 1) * P], y_norm[layer][:, i, :], ident[:, :])
                mm.then_inc(yt_psum_ready[layer], 1)

            def project_out(b, g):
                pe.wait_ge(yt_free[0], group_no(b, g) + 2)
                pe.wait_ge(x1_ready, group_no(b, g) + 1)
                pe.matmul(proj_ps[:, :], w_out[:, :], y_t[:, :], start=True, stop=True)\
                    .then_inc(proj_psum_ready, 1)

            def head(live, g, nxt, finish):
                images = dict(live)
                hooks = {kt: {} for kt in range(HEAD)}
                hooks[0]["clear"] = True
                if finish:
                    if 1 in images:
                        hooks[1][3] = lambda: turn_rows(live, 1, g - 1)
                    if 0 in images:
                        hooks[2][1] = lambda: turn_rows(live, 0, g - 1)
                        hooks[3][1] = lambda: project_out(images[0], g - 1)
                for kt in range(HEAD):
                    steps(live, g, kt, nxt, hooks[kt])

            def rest(live, g, nxt, nxt2):
                with pe.Fori(HEAD, NK - 1) as kt:
                    steps(live, g, kt, nxt)
                last_steps(live, g, nxt, nxt2)

            def project_image(j):
                cols = bass.ds(j * GROUP, GROUP)
                for ps, (c0, c1), done in ((theta_ps, WCOLS[0], theta_psum_ready),
                                           (phi_ps, WCOLS[1], phi_psum_ready)):
                    pe.matmul(ps[0:S0, :], w16[:, 0, c0:c1], x16[:, cols], start=True, stop=False)
                    pe.matmul(ps[0:S0, :], w16[:, 1, c0:c1], x16[:, cols], start=False, stop=True)\
                        .then_inc(done, 1)

            def project_values(layer, j):
                stack, ps, (c0, c1) = ((x16, v0_ps, WCOLS[2]), (q1a, v1_ps, WCOLS[3]))[layer]
                w = c1 - c0
                for i in range(PER):
                    tokens = bass.ds(j * GROUP + i * P, P)
                    pe.matmul(ps[:, i * w:(i + 1) * w], stack[:, tokens], w16[:, 0, c0:c1],
                              start=True, stop=False)
                    mm = pe.matmul(ps[:, i * w:(i + 1) * w], stack[:, tokens], w16[:, 1, c0:c1],
                                   start=False, stop=True)
                mm.then_inc(v_psum_ready[layer], 1)

            def row_tiles(live, g, kt):
                for i in range(PER):
                    for layer, b in live:
                        row_tile(b, layer, g, kt, i, spare=True)

            def fill(live):
                images = dict(live)

                def tile(j, rows):
                    if 0 in images:
                        n = group_no(images[0], j)
                        pe.wait_ge(x16_ready, n + 1)
                        pe.wait_ge(phi_ready, n + 1)
                        project_image(j)
                        pe.wait_ge(v_ready[0], n + 1)
                        project_values(0, j)
                    if 1 in images:
                        n = group_no(images[1], j)
                        pe.wait_ge(x1_lo_ready, n + 2)
                        pe.wait_ge(v_ready[1], n + 1)
                        project_values(1, j)
                    if rows:
                        if 0 in images:
                            pe.wait_ge(stack0_ready, group_no(images[0], j) + 1)
                        if 1 in images:
                            pe.wait_ge(q1b_cleared, images[1] + 1)
                        row_tiles(live, 0, j - 1)

                for layer, b in live:
                    pe.wait_ge(acc_free[layer], group_no(b, 0) + 1)
                for layer, b in live:
                    pe.wait_ge(yt_free[layer], group_no(b, 0) + 1)
                if 0 in images:
                    pe.wait_ge(x1_ready, group_no(images[0], 0) + 1)
                pe.sem_inc(y_seen, 1)
                tile(0, False)
                with pe.Fori(1, NK) as j:
                    tile(j, True)
                if 0 in images:
                    pe.wait_ge(stack0_ready, group_no(images[0] + 1, 0) + 1)
                row_tiles(live, 0, NK - 1)
                if 0 in images:
                    for t in range(BC):
                        row_bank(images[0], 0, t)
                for layer, b in live:
                    pe.wait_ge(v_ready[layer], group_no(b + 1, 0) + 1)

            def passes(live):
                for layer, b in live:
                    turn_maxima(live, layer, 0)
                for i in range(PER):
                    for layer, b in live:
                        row_tile(b, layer, 1, 0, i)
                        if i == 1:
                            pe.wait_ge(max_rows_ready[layer], group_no(b, 0) + 1)
                            col_tile(b, layer, 0, 0, 0)
                        if i == 3:
                            pe.wait_ge(exp_ready[layer], tile0(b, layer, 0) + 1)
                            col_tile(b, layer, 0, 0, 1)
                head(live, 0, True, False)
                with pe.Fori(0, NG - 2) as g:
                    rest(live, g, True, True)
                    head(live, g + 1, True, True)
                rest(live, NG - 2, True, False)
                head(live, NG - 1, False, True)
                rest(live, NG - 1, False, False)
                for layer, b in live:
                    turn_rows(live, layer, NG - 1)
                    if layer == 0:
                        project_out(b, NG - 1)

            def round_of(live):
                fill(live)
                passes(live)

            pe.wait_ge(weights_loaded, WEIGHTS_IN)
            pe.wait_ge(consts_set, CONSTS)
            pe.wait_ge(setup_step, SETUP)
            round_of([(0, 0)])
            with pe.Fori(0, B - 1) as b:
                round_of([(1, b), (0, b + 1)])
            round_of([(1, B - 1)])

        @block.scalar
        def _(act):
            def exp_tile(b, layer, g, kt, c):
                n = tile0(b, layer, g) + kt * PER + c + 1
                act.wait_ge(col_ready[layer], n)
                act.wait_ge(exp_free[layer], n)
                by = (logit[:, 0:1], scales1[:, LOGIT1])[layer]
                act.activation(w_exp[layer][:, c % PER, :], col_bank_of(b, layer, c), ACT.Exp,
                               scale=by).then_inc(exp_ready[layer], 1)

            def exp_bank(b, g, c):
                n = tile0(b, 0, g) + NC + c + 1
                act.wait_ge(col_ready[0], n)
                act.wait_ge(exp_free[0], n)
                act.activation(e_bank[:, c, :], col_bank_of(b, 0, c), ACT.Exp,
                               scale=logit[:, 1:2]).then_inc(exp_ready[0], 1)

            def max_rows(b, layer, g):
                act.wait_ge(max_psum_ready[layer], group_no(b, g) + 1)
                cols = bass.ds(g * GROUP, GROUP)
                if layer == 0:
                    act.activation(q0[S0:R0, cols], turn_ps[S0:R0, :], ACT.Copy).then_inc(max_rows_ready[0], 1)
                else:
                    act.activation(q1b[C:R1, cols], turn_ps[C:R1, :], ACT.Copy).then_inc(max_rows_ready[1], 1)

            def bank_max_rows():
                act.activation(bank_max[C:C + 2, :], turn_ps[C:C + 2, :], ACT.Copy).then_inc(bank_max_ready, 1)

            def take_sums(b, layer, g):
                act.wait_ge(exp_free[layer], tile0(b, layer, g) + T[layer] + PER)
                act.wait_ge(y_ready[layer], group_no(b, g) + 1)
                act.activation(acc_sb[layer][:, 0:ACC[layer]], acc_ps[layer][:, 0:ACC[layer]], ACT.Copy)\
                    .then_inc(acc_free[layer], 1)

            def group(live, g, nxt):
                with act.Fori(0, NK - 1) as kt:
                    for c in range(2, PER + 2):
                        for layer, b in live:
                            exp_tile(b, layer, g, kt, c)
                order = last_order(live)
                for n, (layer, b, s) in enumerate(order):
                    if len(live) == 2 and n == len(order) - 1:
                        take_sums(dict(live)[1], 1, g)
                    tile = s + 2
                    if nxt and tile == T[layer] - 1:
                        max_rows(b, layer, g + 1)
                    if tile < NC:
                        exp_tile(b, layer, g, NK - 1, tile - NC + PER)
                    elif tile < T[layer]:
                        exp_bank(b, g, tile - NC)
                    elif nxt:
                        exp_tile(b, layer, g + 1, 0, tile - T[layer])
                    if nxt and layer == 0 and tile == T[0]:
                        bank_max_rows()
                if len(live) == 2:
                    take_sums(dict(live)[0], 0, g)
                else:
                    (layer, b), = live
                    take_sums(b, layer, g)

            def passes(live):
                for layer, b in live:
                    max_rows(b, layer, 0)
                    if layer == 0:
                        bank_max_rows()
                for tile in range(2):
                    for layer, b in live:
                        exp_tile(b, layer, 0, 0, tile)
                with act.Fori(0, NG - 1) as g:
                    group(live, g, True)
                group(live, NG - 1, False)

            def fill(live):
                images = dict(live)

                def image_hi(j):
                    cols = bass.ds(j * GROUP, GROUP)
                    act.activation(x16[:, cols], x_sb[:, cols], ACT.Copy, scale=scale0[:, 3:4])\
                        .then_inc(x_hi_ready, 1)

                def x1_hi(j):
                    cols = bass.ds(j * GROUP, GROUP)
                    n = group_no(images[1], j)
                    act.wait_ge(x1_ready, n + 2)
                    act.wait_ge(x1_lo_ready, n + 1)
                    by = scales1[:, 0:1]
                    act.activation(k1a[:, cols], x1[:, cols], ACT.Copy, scale=by)
                    act.activation(x1_full[:, :], x1[:, cols], ACT.Copy, scale=by)
                    act.activation(q1a[0:C, cols], x1[0:C, cols], ACT.Copy, scale=by[0:C])
                    act.activation(q1b[0:C, cols], x1[0:C, cols], ACT.Copy, scale=by[0:C])\
                        .then_inc(x1_hi_ready, 1)

                def tile(j, more):
                    cols = bass.ds(j * GROUP, GROUP)
                    if 0 in images:
                        if more:
                            image_hi(j + 1)
                        n = group_no(images[0], j)
                        for i, (ps, stack, come, done) in enumerate(
                                ((theta_ps, q0, theta_psum_ready, theta_ready),
                                 (phi_ps, k0, phi_psum_ready, phi_ready))):
                            act.wait_ge(come, n + 1)
                            if i == 0:
                                act.wait_ge(stack0_ready, n + 1)
                            act.activation(full32[:, i, :], ps[0:S0, :], ACT.Identity,
                                           scale=factor[0:S0, i:i + 1], bias=b_scaled[0:S0, i:i + 1])
                            act.activation(stack[0:S0, cols], ps[0:S0, :], ACT.Identity,
                                           scale=factor[0:S0, i:i + 1], bias=b_scaled[0:S0, i:i + 1])\
                                .then_inc(done, 1)
                    if 1 in images:
                        act.wait_ge(v_psum_ready[1], group_no(images[1], j) + 1)
                        act.activation(v32[1][:, :], v1_ps[:, 0:PER * C], ACT.Copy, scale=scales1[:, FACTOR1])\
                            .then_inc(v32_ready[1], 1)
                        if more:
                            x1_hi(j + 1)

                if 0 in images:
                    act.wait_ge(scale0_ready, images[0] + 1)
                    image_hi(0)
                if 1 in images:
                    act.wait_ge(scale1_ready, images[1] + 2)
                    x1_hi(0)
                with act.Fori(0, NK - 1) as j:
                    tile(j, True)
                tile(NK - 1, False)

            def round_of(live):
                fill(live)
                passes(live)

            round_of([(0, 0)])
            with act.Fori(0, B - 1) as b:
                round_of([(1, b), (0, b + 1)])
            round_of([(1, B - 1)])

        @block.gpsimd
        def _(pool):
            def split(b, layer, g, kt, c):
                pool.wait_ge(exp_ready[layer], tile0(b, layer, g) + kt * PER + c + 1)
                pool.tensor_tensor(w_rest[layer][:, c, :], w_exp[layer][:, c, :],
                                   upper(exp_upper[layer], c, 0, GROUP), ALU.subtract).then_inc(split_p[layer], 1)

            def group(live, g, last=False):
                images = dict(live)

                def tile(kt):
                    for c in range(PER):
                        for layer, b in live:
                            if c in POOL_CHUNKS[share_of(b, layer, g)]:
                                split(b, layer, g, kt, c)

                with pool.Fori(0, NK - 1) as kt:
                    tile(kt)
                if last and 0 in images:
                    peak_over_partitions(images[0] + 1)
                tile(NK - 1)
                if 0 in images:
                    pool.wait_ge(exp_ready[0], tile0(images[0], 0, g) + NC + 1)
                    pool.tensor_tensor(e_bank_rest[:, 0, :], e_bank[:, 0, :], upper(bank_upper, 0, 0, GROUP),
                                       ALU.subtract).then_inc(split_p[0], 1)

            def peak_over_partitions(b):
                pool.wait_ge(peak_ready, b + 1)
                pool.sem_inc(peak_seen, 1)
                pool.partition_all_reduce(peak_all[:, :], peak[:, :], P, RMAX).then_inc(peak_all_ready, 1)

            def round_of(live):
                images = dict(live)

                def x1_lo(j, alone):
                    cols = bass.ds(j * GROUP, GROUP)
                    if not alone:
                        pool.wait_ge(stack0_ready, group_no(images[0], j) + 1)
                    pool.wait_ge(x1_hi_ready, group_no(images[1], j) + 1)
                    pool.tensor_tensor(k1b[0:C, cols], x1_full[0:C, :], k1a[0:C, cols], ALU.subtract)
                    pool.tensor_tensor(q1a[C:P, cols], x1_full[C:P, :], k1a[C:P, cols], ALU.subtract)\
                        .then_inc(x1_lo_ready, 1)

                def stack0_lo(j):
                    cols = bass.ds(j * GROUP, GROUP)
                    n = group_no(images[0], j)
                    if 1 in images:
                        pool.wait_ge(x1_lo_ready, group_no(images[1], j) + 2)
                    pool.wait_ge(theta_ready, n + 1)
                    pool.tensor_tensor(q0[I:2 * I, cols], full32[I:2 * I, 0, :], q0[I:2 * I, cols],
                                       ALU.subtract)
                    pool.wait_ge(phi_ready, n + 2)
                    pool.tensor_tensor(k0[2 * I:S0, cols], full32[2 * I:S0, 1, :], k0[2 * I:S0, cols],
                                       ALU.subtract).then_inc(stack0_ready, 1)

                if 1 in images:
                    pool.wait_ge(split_p[0], NG * splits_of(1, EASY)
                                 + images[1] * ((NG - 1) * splits_of(1, 0) + splits_of(1, EASY)))
                    pool.sem_inc(clear_seen, 1)
                    x1_lo(0, True)
                    pool.wait_ge(acc_free[1], group_no(images[1], 0) + 1)
                    pool.wait_ge(x1_lo_ready, group_no(images[1], 0) + 2)
                    pool.sem_inc(clear_seen, 1)
                    pool.memset(q1b[C:R1, :], 0.0).then_inc(q1b_cleared, 1)
                    pool.wait_ge(q1b_cleared, images[1] + 1)
                    pool.sem_inc(clear_seen, 1)
                with pool.Fori(0, NK - 1) as j:
                    if 0 in images:
                        stack0_lo(j)
                    if 1 in images:
                        x1_lo(j + 1, 0 not in images)
                if 0 in images:
                    stack0_lo(NK - 1)
                with pool.Fori(0, NG - 1) as g:
                    group(live, g)
                group(live, NG - 1, last=True)

            pool.wait_ge(stats_ready, 8)
            pool.partition_all_reduce(stat_all[:, :], stat[:, :], P, RMAX).then_inc(stats_all_ready, 1)
            peak_over_partitions(0)
            round_of([(0, 0)])
            with pool.Fori(0, B - 1) as b:
                round_of([(1, b), (0, b + 1)])
            round_of([(1, B - 1)])

        @block.vector
        def _(v):
            def powers(peaks, width):
                bits = peaks.bitcast(U32)
                v.tensor_scalar(pow_dn[:, 0:width].bitcast(U32), bits, EXPONENT, None, ALU.bitwise_and)
                return v.tensor_scalar(pow_up[:, 0:width].bitcast(U32), bits, EXPONENT, EXPONENT,
                                       ALU.bitwise_xor, ALU.bitwise_and)

            def peak_of_group(g):
                v.tensor_reduce(peak_part[:, bass.ds(g, 1)], x_sb[:, bass.ds(g * GROUP, GROUP)], AX_X, ALU.max,
                                apply_absolute_value=True).then_inc(peak_part_ready, 1)

            def peak_of_next(b, g):
                v.wait_ge(x_loaded, (b * (NG - 1) + g + 1) * 32)
                peak_of_group(g)

            def image_scales(b):
                n = b * 11
                v.wait_ge(peak_part_ready, group_no(b + 1, 0))
                v.tensor_reduce(peak[:, :], peak_part[:, :], AX_X, ALU.max).then_inc(peak_ready, 1)
                v.wait_ge(peak_all_ready, b + 1)
                v.scalar_tensor_tensor(bound[:, 0:3], stat_all[:, 0:3], peak_all[:, 0:1], stat_all[:, 6:9],
                                       ALU.mult, ALU.add).then_inc(scale_step, 1)
                v.tensor_copy(bound[:, 3:4], peak_all[:, :]).then_inc(scale_step, 1)
                v.wait_ge(scale_step, n + 2)
                v.scalar_tensor_tensor(bound[:, 4:5], bound[:, 2:3], stat_all[:, 4:5], out_const[:, :],
                                       ALU.mult, ALU.add).then_inc(scale_step, 1)
                v.wait_ge(scale_step, n + 3)
                v.tensor_tensor(bound[:, 4:5], bound[:, 4:5], peak_all[:, :], ALU.add).then_inc(scale_step, 1)
                v.wait_ge(scale_step, n + 4)
                v.tensor_tensor(bound[:, 5:6], bound[:, 4:5], stat_all[:, 3:4], ALU.mult).then_inc(scale_step, 1)
                v.wait_ge(scale_step, n + 5)
                v.tensor_scalar(bound[:, :], bound[:, :], TINY, None, ALU.max).then_inc(scale_step, 1)
                v.wait_ge(scale_step, n + 6)
                powers(bound[:, :], 6).then_inc(scale_step, 1)
                v.wait_ge(scale_step, n + 7)
                scale0, inv0, factor, b_scaled, logit, lift = layer0_scales(scales_next)
                scales1_next = scales_next[:, SCALES - 7:]
                sc1, inv1 = scales1_next[:, SC1], scales1_next[:, INV1]
                v.tensor_scalar(scale0[:, :], pow_up[:, 0:4], 4.0, None, ALU.mult)
                v.tensor_scalar(inv0[:, :], pow_dn[:, 0:4], 0.125, None, ALU.mult)
                v.tensor_scalar(sc1, pow_up[:, 4:6], 4.0, None, ALU.mult)
                v.tensor_scalar(inv1, pow_dn[:, 4:6], 0.125, None, ALU.mult).then_inc(scale_step, 1)
                v.wait_ge(scale_step, n + 8)
                v.scalar_tensor_tensor(factor[:, :], scale0[:, 0:3], inv0[:, 3:4], w_i[:, 0:3],
                                       ALU.mult, ALU.mult)
                v.scalar_tensor_tensor(scales1_next[:, FACTOR1], sc1[:, 1:2], inv1[:, 0:1], w_i[:, 3:4],
                                       ALU.mult, ALU.mult)
                v.tensor_tensor(b_scaled[:, :], b_stat[:, 0:2], scale0[:, 0:2], ALU.mult)
                v.tensor_tensor(logit[:, 0:1], inv0[:, 0:1], inv0[:, 1:2], ALU.mult)
                v.scalar_tensor_tensor(logit[:, 1:2], inv0[:, 1:2], BANK_SCALE, w_i[:, 4:5],
                                       ALU.mult, ALU.mult)
                v.tensor_tensor(scales1_next[:, LOGIT1], inv1[:, 0:1], inv1[:, 0:1], ALU.mult)
                v.scalar_tensor_tensor(lift[:, 0:1], scale0[:, 0:1], LIFT, scale0[:, 1:2],
                                       ALU.mult, ALU.mult).then_inc(scale_step, 1)
                v.scalar_tensor_tensor(lift[:, 1:2], scale0[:, 1:2], LIFT / BANK_SCALE, w_s[:, 4:5],
                                       ALU.mult, ALU.mult)
                v.scalar_tensor_tensor(scales1_next[:, LIFT1], sc1[:, 0:1], LIFT, sc1[:, 0:1],
                                       ALU.mult, ALU.mult).then_inc(scale_step, 1)
                v.wait_ge(scale_step, n + 10)
                v.tensor_scalar(lift[:, :], lift[:, :], LIFT_MOST, None, ALU.min)
                v.tensor_scalar(scales1_next[:, LIFT1], scales1_next[:, LIFT1], LIFT_MOST, None, ALU.min)\
                    .then_inc(scale_step, 1)

            def take_scales(b):
                v.wait_ge(scale_step, (b + 1) * 11)
                v.tensor_copy(scales1[:, :], scales_now[:, SCALES - 7:]).then_inc(scale1_ready, 1)
                v.wait_ge(scale1_ready, b + 1)
                v.tensor_copy(scales_now[:, :], scales_next[:, :]).then_inc(scale0_ready, 1)
                v.wait_ge(scale0_ready, b + 1)
                v.tensor_scalar(g_bias_scaled[:, :], g_bias[:, :], scale0[:, 2:3], None, ALU.mult)

            def values(b, layer, j):
                n = group_no(b, j)
                w = (I, C)[layer]
                here = v32[layer][:, :]
                if layer == 0:
                    v.wait_ge(v_psum_ready[0], n + 1)
                    v.scalar_tensor_tensor(here, v0_ps[:, 0:PER * w], factor[:, 2:3], g_bias_scaled[:, :],
                                           ALU.mult, ALU.add).then_inc(v32_ready[0], 1)
                v.wait_ge(v32_ready[layer], n + 1)
                here = here.rearrange("p (i c) -> p i c", c=w)
                chunks = bass.ds(j * PER, PER)
                dst = (v0, v1)[layer]
                lo = (I, C + 1)[layer]
                v.tensor_copy(dst[:, chunks, 0:w], here).then_inc(v_hi_ready[layer], 1)
                v.wait_ge(v_hi_ready[layer], n + 1)
                v.tensor_tensor(dst[:, chunks, lo:lo + w], here, dst[:, chunks, 0:w], ALU.subtract)\
                    .then_inc(v_ready[layer], 1)

            def row_max(b, layer, g, kt, i, spare=False):
                v.wait_ge(row_ready[layer], tile0(b, layer, g) + kt * PER + i + 1)
                v.tensor_reduce(max_part[layer][:, i, bass.ds(kt, 1)], row_bank_of(b, layer, i, spare), AX_X, ALU.max)\
                    .then_inc(row_free[layer], 1)

            def bank_row_max(b, g, t):
                v.wait_ge(row_ready[0], tile0(b, 0, g) + NC + t + 1)
                v.tensor_reduce(neg_max[0][:, PER + 2 * t:PER + 2 * t + 2],
                                row_bank_of(b, 0, t, False).rearrange("p (i k) -> p i k", k=BANK),
                                AX_X, ALU.max, negate=True).then_inc(row_free[0], 1)

            def group_maxima(b, layer, g):
                n = group_no(b, g)
                v.wait_ge(row_free[layer], tile0(b, layer, g) + T[layer] + 2)
                v.tensor_reduce(neg_max[layer][:, 0:PER], max_part[layer][:, :, :], AX_X, ALU.max, negate=True)\
                    .then_inc(neg_max_ready[layer], 1)
                v.wait_ge(neg_max_ready[layer], n + 1)
                if layer == 0:
                    spans = [(0, PER, lift[:, 0:1]), (PER, 2 * PER, lift[:, 1:2])]
                else:
                    spans = [(0, PER, scales1[:, LIFT1])]
                for a, e, up in spans:
                    op = v.tensor_scalar(max_cols[layer][:, a:e, 0], neg_max[layer][:, a:e], up, None, ALU.add)
                op.then_inc(max_hi_ready[layer], 1)
                v.wait_ge(max_hi_ready[layer], n + 1)
                for a, e, up in spans:
                    op = v.scalar_tensor_tensor(max_cols[layer][:, a:e, 1], neg_max[layer][:, a:e], up,
                                                max_cols[layer][:, a:e, 0], ALU.add, ALU.subtract)
                op.then_inc(max_cols_ready[layer], 1)

            def split_after(b, layer, g, kt, c):
                if c + 1 == PER or c + 1 in POOL_CHUNKS[share_of(b, layer, g)]:
                    return
                v.wait_ge(exp_ready[layer], tile0(b, layer, g) + kt * PER + c + 2)
                v.tensor_tensor(w_rest[layer][:, c + 1, :], w_exp[layer][:, c + 1, :],
                                upper(exp_upper[layer], c + 1, 0, GROUP), ALU.subtract).then_inc(split_v[layer], 1)

            def steps(live, g, kt, nxt, after=None):
                for c in range(PER):
                    for layer, b in live:
                        if nxt:
                            row_max(b, layer, g + 1, kt + 1, c)
                        split_after(b, layer, g, kt, c)
                    if after and c in after:
                        after[c]()

            def last_steps(live, g, nxt, nxt2):
                kt = NK - 1
                for layer, b, s in last_order(live):
                    rows_from = T[layer] - PER
                    if s < rows_from and nxt:
                        bank_row_max(b, g + 1, s - kt * PER)
                    if s == rows_from and nxt:
                        group_maxima(b, layer, g + 1)
                    if s >= rows_from and nxt2:
                        row_max(b, layer, g + 2, 0, s - rows_from)
                    if s < NC:
                        split_after(b, layer, g, kt, s - kt * PER)
                    elif s == NC:
                        v.wait_ge(exp_ready[0], tile0(b, 0, g) + NC + 2)
                        v.tensor_tensor(e_bank_rest[:, 1, :], e_bank[:, 1, :], upper(bank_upper, 1, 0, GROUP),
                                        ALU.subtract).then_inc(split_v[0], 1)

            def normalise(b, layer, g):
                n = group_no(b, g)
                v.wait_ge(acc_free[layer], n + 2)
                by = recip[layer][:, 0:PER].unsqueeze(2)
                if layer:
                    w = 2 * C + 1
                    wide = acc_sb[1][:, 0:WIDE * w].rearrange("p (q w) -> p q w", w=w)
                    one = acc_sb[1][:, WIDE * w:].rearrange("p (q w) -> p q w", w=C + 1)
                    half = y_sum1[:, :].rearrange("p (q c) -> p q c", c=C)
                    v.reciprocal(recip[1][:, 0:WIDE], wide[:, :, C])
                    v.reciprocal(recip[1][:, WIDE:PER], one[:, :, C]).then_inc(norm_step[1], 1)
                    v.tensor_tensor(half, wide[:, :, 0:C], wide[:, :, C + 1:], ALU.add).then_inc(norm_step[1], 1)
                    v.wait_ge(norm_step[1], 2 * n + 2)
                    v.scalar_tensor_tensor(y_norm[1][:, 0:WIDE, :], half, scales1[:, 3:4],
                                           by[:, 0:WIDE].broadcast_to([P, WIDE, C]), ALU.mult, ALU.mult)
                    v.scalar_tensor_tensor(y_norm[1][:, WIDE:, :], one[:, :, 0:C], scales1[:, 3:4],
                                           by[:, WIDE:].broadcast_to([P, 1, C]), ALU.mult, ALU.mult)\
                        .then_inc(y_ready[1], 1)
                    return
                w = MAIN[0]
                main = acc_sb[0][:, 0:PER * w].rearrange("p (q w) -> p q w", w=w)
                side = acc_sb[0][:, PER * w:].rearrange("p (q w) -> p q w", w=BANKW)
                half = y_sum[:, :].rearrange("p (q c) -> p q c", c=I)
                v.reciprocal(recip[0][:, 0:PER], main[:, :, 2 * I])
                v.reciprocal(recip[0][:, PER:], side[:, :, I]).then_inc(norm_step[0], 1)
                v.tensor_tensor(half, main[:, :, 0:I], main[:, :, I:2 * I], ALU.add).then_inc(norm_step[0], 1)
                v.wait_ge(norm_step[0], 2 * n + 2)
                v.scalar_tensor_tensor(y_norm[0][:, :, 0:I], half, inv0[:, 2:3],
                                       by.broadcast_to([P, PER, I]), ALU.mult, ALU.mult)
                v.scalar_tensor_tensor(y_norm[0][:, :, I:C], side[:, :, 0:I], w_i[:, 4:5],
                                       recip[0][:, PER:].unsqueeze(2).broadcast_to([P, PER, I]),
                                       ALU.mult, ALU.mult).then_inc(y_ready[0], 1)

            def take_rows(b, layer, g):
                v.wait_ge(yt_psum_ready[layer], group_no(b, g) + 1)
                cols = bass.ds(g * GROUP, GROUP)
                if layer == 0:
                    v.tensor_copy(y_t[:, :], turn_ps[0:C, :]).then_inc(yt_free[0], 1)
                else:
                    v.tensor_tensor(out_sb[:, cols], turn_ps[0:C, :], x1[0:C, cols], ALU.add)\
                        .then_inc(yt_free[1], 1)

            def add_image(b, g, last=False):
                cols = bass.ds(g * GROUP, GROUP)
                image = x_keep[:, :] if last else x_sb[:, cols]
                v.wait_ge(proj_psum_ready, group_no(b, g) + 1)
                v.scalar_tensor_tensor(x1[:, cols], proj_ps[:, :], b_out[:, :], image,
                                       ALU.add, ALU.add).then_inc(x1_ready, 1)

            def head(live, g, nxt, finish):
                images = dict(live)
                hooks = {kt: {} for kt in range(HEAD)}
                if finish:
                    if 1 in images:
                        hooks[0][3] = lambda: normalise(images[1], 1, g - 1)
                        hooks[2][0] = lambda: take_rows(images[1], 1, g - 1)
                    if 0 in images:
                        hooks[1][1] = lambda: normalise(images[0], 0, g - 1)
                        hooks[3][0] = lambda: take_rows(images[0], 0, g - 1)
                        hooks[3][3] = lambda: add_image(images[0], g - 1)
                        hooks[4][3] = lambda: peak_of_next(images[0] + 1, g - 1)
                for kt in range(HEAD):
                    steps(live, g, kt, nxt, hooks[kt])

            def rest(live, g, nxt, nxt2):
                with v.Fori(HEAD, NK - 1) as kt:
                    steps(live, g, kt, nxt)
                if not nxt and 0 in dict(live):
                    next_image = dict(live)[0] + 1
                    v.wait_ge(x_last_loaded, (next_image + 1) * 32)
                    peak_of_group(NG - 1)
                    image_scales(next_image)
                last_steps(live, g, nxt, nxt2)

            def passes(live):
                head(live, 0, True, False)
                with v.Fori(0, NG - 2) as g:
                    rest(live, g, True, True)
                    head(live, g + 1, True, True)
                rest(live, NG - 2, True, False)
                images = dict(live)
                if 0 in images:
                    v.tensor_copy(x_keep[:, :], x_sb[:, (NG - 1) * GROUP:]).then_inc(image_kept, 1)
                head(live, NG - 1, False, True)
                rest(live, NG - 1, False, False)
                for layer, b in live:
                    normalise(b, layer, NG - 1)
                if 0 in images:
                    take_scales(images[0] + 1)
                for layer, b in live:
                    take_rows(b, layer, NG - 1)
                if 0 in images:
                    add_image(images[0], NG - 1, last=True)

            def row_maxima(live, g, kt, spare):
                for i in range(PER):
                    for layer, b in live:
                        row_max(b, layer, g, kt, i, spare)

            def fill(live):
                images = dict(live)

                def image_lo(j):
                    cols = bass.ds(j * GROUP, GROUP)
                    v.wait_ge(x_hi_ready, group_no(images[0], j) + 1)
                    v.scalar_tensor_tensor(x16[C:P, cols], x_sb[C:P, cols], scale0[C:P, 3:4], x16[C:P, cols],
                                           ALU.mult, ALU.subtract).then_inc(x16_ready, 1)

                def tile(j, rows, more):
                    if 0 in images:
                        if more:
                            image_lo(j + 1)
                        values(images[0], 0, j)
                    if rows:
                        row_maxima(live, 0, j - 1, True)
                    if 1 in images:
                        values(images[1], 1, j)

                if 0 in images:
                    image_lo(0)
                if 1 in images:
                    v.wait_ge(out_stored, (group_no(images[1], 0) + 1) * 16)
                tile(0, False, True)
                with v.Fori(1, NK - 1) as j:
                    tile(j, True, True)
                tile(NK - 1, True, False)
                row_maxima(live, 0, NK - 1, True)
                if 0 in images:
                    for t in range(BC):
                        bank_row_max(images[0], 0, t)
                for layer, b in live:
                    group_maxima(b, layer, 0)
                row_maxima(live, 1, 0, False)

            def round_of(live):
                fill(live)
                passes(live)

            v.memset(ones2[C:C + 2, :], 1.0).then_inc(consts_set, 1)
            v.memset(zero16[:, :], 0.0).then_inc(consts_set, 1)
            v.memset(k0[S0:R0, :], 1.0).then_inc(consts_set, 1)
            v.memset(k1b[C:R1, :], 1.0).then_inc(consts_set, 1)
            v.memset(v0[:, :, 2 * I:2 * I + 1], 1.0).then_inc(consts_set, 1)
            v.memset(v1[:, :, C:C + 1], 1.0).then_inc(consts_set, 1)
            v.memset(bank_val[:, :, I:I + 1], 1.0).then_inc(consts_set, 1)
            for layer in range(2):
                for free, count in ((row_free, 2), (exp_free, PER), (acc_free, 1), (y_ready, 1), (yt_free, 1),
                                    (v_ready, 1)):
                    v.sem_inc(free[layer], count)
            for free in (x1_ready, stack0_ready, x1_lo_ready, phi_ready):
                v.sem_inc(free, 1)
            v.wait_ge(weights_loaded, WEIGHTS_IN)
            v.tensor_copy(ident16[:, :], ident[:, :]).then_inc(consts_set, 1)
            v.tensor_tensor(b_out[:, :], b_out2[:, 0:1], b_out2[:, 1:2], ALU.add).then_inc(consts_set, 1)
            v.tensor_reduce(stat[:, 0:6], w_stat[:, :, :], AX_X, ALU.add, apply_absolute_value=True)\
                .then_inc(stats_ready, 1)
            v.tensor_reduce(stat[:, 6:11], b_stat[:, :].unsqueeze(2), AX_X, ALU.max,
                            apply_absolute_value=True).then_inc(stats_ready, 1)
            v.tensor_reduce(stat[:, 11:15], w_stat[:, 0:4, :], AX_X, ALU.max, apply_absolute_value=True)\
                .then_inc(stats_ready, 1)
            v.tensor_reduce(stat[:, 15:16], bank[:, :], AX_X, ALU.max, apply_absolute_value=True)\
                .then_inc(stats_ready, 5)
            v.wait_ge(stats_all_ready, 1)
            v.tensor_tensor(out_const[:, :], stat_all[:, 15:16], stat_all[:, 5:6], ALU.mult)\
                .then_inc(setup_step, 1)
            v.wait_ge(setup_step, 1)
            for n in (9, 10):
                v.tensor_tensor(out_const[:, :], out_const[:, :], stat_all[:, n:n + 1], ALU.add)\
                    .then_inc(setup_step, 1)
                v.wait_ge(setup_step, n - 7)
            v.tensor_scalar(w_clamp[:, :], stat_all[:, 11:16], TINY, None, ALU.max).then_inc(setup_step, 1)
            v.wait_ge(setup_step, 4)
            powers(w_clamp[:, :], 5).then_inc(setup_step, 1)
            v.wait_ge(setup_step, 5)
            v.tensor_scalar(w_s[:, :], pow_up[:, 0:5], 4.0, None, ALU.mult)
            v.tensor_scalar(w_i[:, :], pow_dn[:, 0:5], 0.125, None, ALU.mult).then_inc(setup_step, 1)
            v.wait_ge(setup_step, 6)
            for n, (c0, c1) in enumerate(WCOLS):
                v.tensor_scalar(w_scaled[:, c0:c1], w_proj[:, c0:c1], w_s[:, n:n + 1], None, ALU.mult)
            v.tensor_scalar(bank_t[:, :, :], bank_t[:, :, :], w_s[:, 4:5], None, ALU.mult)
            v.tensor_scalar(bank32[:, :], bank[:, :], w_s[:, 4:5], None, ALU.mult).then_inc(setup_step, 1)
            v.wait_ge(setup_step, 7)
            v.tensor_copy(w16[:, 0, :], w_scaled[:, :])
            v.tensor_copy(bank_val[:, :, 0:I], bank_t[:, :, :])
            v.tensor_copy(bank_stack[:, :], bank32[:, :]).then_inc(setup_step, 1)
            v.wait_ge(setup_step, 8)
            v.tensor_tensor(w16[:, 1, :], w_scaled[:, :], w16[:, 0, :], ALU.subtract)
            v.tensor_tensor(bank_val[:, :, I + 1:], bank_t[:, :, :], bank_val[:, :, 0:I],
                            ALU.subtract).then_inc(consts_set, 3)
            v.tensor_tensor(bank_stack[I:2 * I, :], bank32[I:2 * I, :], bank_stack[I:2 * I, :],
                            ALU.subtract).then_inc(setup_step, 1)
            v.wait_ge(x_loaded, (NG - 1) * 32)
            v.wait_ge(x_last_loaded, 32)
            with v.Fori(0, NG) as g:
                peak_of_group(g)
            v.memset(scales_now[:, :], 1.0)
            image_scales(0)
            take_scales(0)
            round_of([(0, 0)])
            with v.Fori(0, B - 1) as b:
                round_of([(1, b), (0, b + 1)])
            round_of([(1, B - 1)])


def kernel(x, L0_conv_g_w, L0_conv_g_b, L0_conv_theta_w, L0_conv_theta_b, L0_conv_phi_w, L0_conv_phi_b,
           L0_conv_W_w, L0_conv_W_b, L0_conv_Wz1_w, L0_conv_Wz1_b, L0_conv_mb, L1_conv_weight):
    import numpy as np
    import concourse.bacc as bacc
    from concourse.bass_utils import run_bass_kernel_spmd

    def a(t):
        return np.asarray(t)

    def rows(t):
        full = np.zeros((P, c), np.float32)
        full[:, :t.shape[1]] = np.tile(t, (P // t.shape[0], 1))
        return full

    nb, c, h, w = x.shape
    inter = L0_conv_g_w.shape[0]
    chunks = L0_conv_mb.shape[1] // P
    theta_t, phi_t = a(L0_conv_theta_w).T, a(L0_conv_phi_w).T
    weights = np.concatenate([theta_t] * 3 + [phi_t] * 3 + [a(L0_conv_g_w).T, a(L1_conv_weight)], axis=1)
    arrays = {
        "x": a(x).reshape(nb, c, h * w),
        "weights": np.tile(weights, (2, 1)),
        "wstat": np.stack([rows(a(t)) for t in (L0_conv_theta_w, L0_conv_phi_w, L0_conv_g_w,
                                                a(L1_conv_weight).T, L0_conv_W_w, L0_conv_Wz1_w)], axis=1),
        "bstat": np.stack([np.tile(a(t), P // t.shape[0]) for t in (
            L0_conv_theta_b, L0_conv_phi_b, L0_conv_g_b, L0_conv_W_b, L0_conv_Wz1_b)], axis=1),
        "out_w": np.concatenate([np.tile(a(L0_conv_W_w).T, (1, 2)), np.tile(a(L0_conv_Wz1_w).T, (1, 2))], axis=0),
        "out_b": np.stack([np.tile(a(L0_conv_W_b), 2), np.tile(a(L0_conv_Wz1_b), 2)], axis=1),
        "g_bias": np.tile(a(L0_conv_g_b), (P, GROUP // P)),
        "bank": np.tile(a(L0_conv_mb), (P // inter, 1)),
        "bank_t": a(L0_conv_mb).T.reshape(chunks, P, inter).transpose(1, 0, 2),
        "ident": np.eye(P, dtype=np.float32),
    }
    arrays = {name: np.ascontiguousarray(t) for name, t in arrays.items()}
    nc = bacc.Bacc("TRN2", target_bir_lowering=False, num_devices=1)
    args = [nc.dram_tensor(f"{name}_dram", t.shape, mybir.dt.from_np(t.dtype), kind="ExternalInput").ap()
            for name, t in arrays.items()]
    out = nc.dram_tensor("out_dram", arrays["x"].shape, F32, kind="ExternalOutput").ap()
    non_local_then_graph(nc, *args, out)
    r = run_bass_kernel_spmd(nc, [{f"{name}_dram": t for name, t in arrays.items()}], core_ids=[0])
    return r.results[0]["out_dram"].reshape(nb, c, h, w)
```
